# Optimizing a Trainium2 kernel written in Bass

```python
import numpy as np
import jax
import jax.numpy as jnp

def _softmax(x, axis=-1):
    return jax.nn.softmax(x, axis=axis)

def _gelu(x):
    return jax.nn.gelu(x, approximate=True)

def _silu(x):
    return jax.nn.silu(x)

def _sigmoid(x):
    return jax.nn.sigmoid(x)

def _layernorm(x, axis=-1, eps=1e-05):
    m = jnp.mean(x, axis=axis, keepdims=True)
    v = jnp.var(x, axis=axis, keepdims=True)
    return (x - m) / jnp.sqrt(v + eps)

def _scatter_add(tgt, idx, src, axis=0):
    return tgt.at[idx].add(src)

def _segment_sum(src, seg, n):
    return jax.ops.segment_sum(src, seg, n)
kernel_name = 'mk_gps_d2_gnn_r8_88d40b'

def setup_inputs(seed: int=0):
    np.random.seed(seed)
    _w = jnp.asarray

    def _rec_inputs():
        import jax
        import jax.numpy as jnp
        _gk = jax.random.key(seed)
        x = -8.776e-05 + 1 * jax.random.normal(jax.random.fold_in(_gk, 1), (1250, 512), jnp.float32)
        _s = jax.random.randint(jax.random.fold_in(_gk, 2), (10000,), 0, 1250, jnp.int32)
        _d = jax.random.randint(jax.random.fold_in(_gk, 3), (10000,), 0, 1250, jnp.int32)
        _loop = jnp.arange(1250, dtype=jnp.int32)
        src = jnp.concatenate([_s, _d, _loop])
        dst = jnp.concatenate([_d, _s, _loop])
        _o = jnp.argsort(dst, stable=True)
        src = src[_o]
        dst = dst[_o]
        edge_weight = jax.random.uniform(jax.random.fold_in(_gk, 13), (21250,), jnp.float32, 0.0, 0.999996)
        return (x, src, dst, edge_weight)
    x, src, dst, edge_weight = _rec_inputs()

    def _L0_gnn_setup():
        import jax, jax.numpy as jnp
        import numpy as np
        N = 1250
        E = 20000
        D_IN = 512
        D_OUT = 512
        key = jax.random.key(seed)
        k1, k2, k3, k4, k5 = jax.random.split(key, 5)
        x = jax.random.normal(k1, (N, D_IN), dtype=jnp.float32)
        edge_index = jax.random.randint(k2, (2, E), 0, N, dtype=jnp.int64)
        edge_attr = jax.random.uniform(k3, (E,), dtype=jnp.float32)
        W = jax.random.normal(k4, (D_IN, D_OUT), dtype=jnp.float32) * 0.05
        b = jax.random.normal(k5, (D_OUT,), dtype=jnp.float32) * 0.05
        return {'x': x, 'edge_index': edge_index, 'edge_attr': edge_attr, 'W': W, 'b': b}
    _L0_gnn_all = _L0_gnn_setup()
    _L0_gnn_in = {k: v for k, v in _L0_gnn_all.items() if k in ('W', 'b')}
    del _L0_gnn_all

    def _L0_mix_setup():
        import jax, jax.numpy as jnp
        import numpy as np
        DIM = 512
        HEADS = 8
        DIM_HEAD = 64
        INNER = HEADS * DIM_HEAD
        key = jax.random.key(seed)
        k1, k2, k3, k4 = jax.random.split(key, 4)
        x = jax.random.normal(k1, (4, 1024, DIM), dtype=jnp.float32)
        w_qkv = jax.random.normal(k2, (DIM, 3 * INNER), dtype=jnp.float32) / np.sqrt(DIM)
        w_out = jax.random.normal(k3, (INNER, DIM), dtype=jnp.float32) / np.sqrt(INNER)
        b_out = jax.random.normal(k4, (DIM,), dtype=jnp.float32) * 0.01
        return {'x': x, 'w_qkv': w_qkv, 'w_out': w_out, 'b_out': b_out}
    _L0_mix_all = _L0_mix_setup()
    _L0_mix_in = {k: v for k, v in _L0_mix_all.items() if k in ('w_qkv', 'w_out', 'b_out')}
    del _L0_mix_all

    def _L0_ffn_setup():
        import jax, jax.numpy as jnp
        import numpy as np
        MARK_AX = 0
        OP_MUL = 1
        OPCODE_BASE = 2
        ALU_LO, ALU_HI = (64, 80)
        AX_CARRY_LO, AX_CARRY_HI = (96, 112)
        OUTPUT_LO, OUTPUT_HI = (128, 144)
        NIB_A, NIB_B, RESULT, OP_START = (0, 1, 2, 3)
        GE_DIM = 160
        N_POS = 8
        N_LAYERS = 7
        OPCODE = 27

        def _decode_nibble(x16):
            return jnp.argmax(x16 > 0.5, axis=-1).astype(x16.dtype)
        key = jax.random.key(seed)
        k1, k2, k3 = jax.random.split(key, 3)
        x_bd = jax.random.uniform(k1, (4, 1024, 512), dtype=jnp.float32)
        W = jax.random.normal(k2, (N_LAYERS, GE_DIM, GE_DIM), dtype=jnp.float32) * 0.05
        b = jax.random.normal(k3, (N_LAYERS, GE_DIM), dtype=jnp.float32) * 0.01
        return {'x_bd': x_bd, 'W': W, 'b': b}
    _L0_ffn_all = _L0_ffn_setup()
    _L0_ffn_in = {k: v for k, v in _L0_ffn_all.items() if k in ('W', 'b')}
    del _L0_ffn_all

    def _L1_gnn_setup():
        import jax, jax.numpy as jnp
        import numpy as np
        N_NODES = 12500
        N_EDGES = 400000
        IN_F = 512
        OUT_F = 512
        RANK = 64
        key = jax.random.key(seed)
        ks = jax.random.split(key, 8)
        inp = jax.random.normal(ks[0], (N_NODES, IN_F), dtype=jnp.float32)
        U = jax.random.normal(ks[1], (IN_F, RANK), dtype=jnp.float32) / np.sqrt(IN_F)
        s = jax.random.uniform(ks[2], (RANK,), dtype=jnp.float32)
        Vt = jax.random.normal(ks[3], (RANK, OUT_F), dtype=jnp.float32) / np.sqrt(RANK)
        bias = jax.random.normal(ks[4], (OUT_F,), dtype=jnp.float32) * 0.01
        edge_row = jax.random.randint(ks[5], (N_EDGES,), 0, N_NODES, dtype=jnp.int64 if jax.config.jax_enable_x64 else jnp.int32)
        edge_col = jax.random.randint(ks[6], (N_EDGES,), 0, N_NODES, dtype=jnp.int64 if jax.config.jax_enable_x64 else jnp.int32)
        edge_val = jax.random.uniform(ks[7], (N_EDGES,), dtype=jnp.float32)
        return {'input': inp, 'U': U, 's': s, 'Vt': Vt, 'bias': bias, 'edge_row': edge_row, 'edge_col': edge_col, 'edge_val': edge_val}
    _L1_gnn_all = _L1_gnn_setup()
    _L1_gnn_in = {k: v for k, v in _L1_gnn_all.items() if k in ('U', 's', 'Vt', 'bias')}
    del _L1_gnn_all

    def _L1_mix_setup():
        import jax, jax.numpy as jnp
        import numpy as np
        NUM_HEADS = 8
        key = jax.random.key(seed)
        k1, k2, k3 = jax.random.split(key, 3)
        B, N, C = (4, 512, 512)
        x = jax.random.normal(k1, (B, N, C), dtype=jnp.float32)
        w_qkv = jax.random.normal(k2, (C, 3 * C), dtype=jnp.float32) * (1.0 / np.sqrt(C))
        w_proj = jax.random.normal(k3, (C, C), dtype=jnp.float32) * (1.0 / np.sqrt(C))
        b_proj = jnp.zeros((C,), dtype=jnp.float32)
        return {'x': x, 'w_qkv': w_qkv, 'w_proj': w_proj, 'b_proj': b_proj}
    _L1_mix_all = _L1_mix_setup()
    _L1_mix_in = {k: v for k, v in _L1_mix_all.items() if k in ('w_qkv', 'w_proj', 'b_proj')}
    del _L1_mix_all

    def _L1_ffn_setup():
        import jax, jax.numpy as jnp
        import numpy as np

        def _haar_dwt2(x):
            a = x[:, ::2, ::2]
            b = x[:, ::2, 1::2]
            c = x[:, 1::2, ::2]
            d = x[:, 1::2, 1::2]
            ll = (a + b + c + d) * 0.5
            lh = (a + b - c - d) * 0.5
            hl = (a - b + c - d) * 0.5
            hh = (a - b - c + d) * 0.5
            return (ll, lh, hl, hh)

        def _haar_idwt2(ll, lh, hl, hh):
            a = (ll + lh + hl + hh) * 0.5
            b = (ll + lh - hl - hh) * 0.5
            c = (ll - lh + hl - hh) * 0.5
            d = (ll - lh - hl + hh) * 0.5
            B, H2, W2 = ll.shape
            out = jnp.zeros((B, 2 * H2, 2 * W2), ll.dtype)
            out = out.at[:, ::2, ::2].set(a)
            out = out.at[:, ::2, 1::2].set(b)
            out = out.at[:, 1::2, ::2].set(c)
            out = out.at[:, 1::2, 1::2].set(d)
            return out

        def _interp_linear_last(x, m):
            n = x.shape[-1]
            pos = jnp.linspace(0.0, 1.0, m, dtype=x.dtype) * (n - 1)
            i0 = jnp.clip(jnp.floor(pos).astype(jnp.int32), 0, n - 2)
            w = pos - i0.astype(x.dtype)
            return x[..., i0] * (1.0 - w) + x[..., i0 + 1] * w
        key = jax.random.key(seed)
        k0, k1, k2 = jax.random.split(key, 3)
        b, f, c, hidden = (128, 256, 512, 256)
        x = jax.random.normal(k0, (b, f, c), dtype=jnp.float32)
        fc1_w = jax.random.normal(k1, (hidden, c), dtype=jnp.float32) * 0.02
        fc1_b = jnp.zeros((hidden,), dtype=jnp.float32)
        fc2_w = jax.random.normal(k2, (c // 2, hidden), dtype=jnp.float32) * 0.02
        fc2_b = jnp.zeros((c // 2,), dtype=jnp.float32)
        return {'x': x, 'fc1_w': fc1_w, 'fc1_b': fc1_b, 'fc2_w': fc2_w, 'fc2_b': fc2_b}
    _L1_ffn_all = _L1_ffn_setup()
    _L1_ffn_in = {k: v for k, v in _L1_ffn_all.items() if k in ('fc1_w', 'fc1_b', 'fc2_w', 'fc2_b')}
    del _L1_ffn_all
    return {'x': x, 'src': src, 'dst': dst, 'edge_weight': edge_weight, 'L0_gnn_W': _L0_gnn_in['W'], 'L0_gnn_b': _L0_gnn_in['b'], 'L0_mix_w_qkv': _L0_mix_in['w_qkv'], 'L0_mix_w_out': _L0_mix_in['w_out'], 'L0_mix_b_out': _L0_mix_in['b_out'], 'L0_ffn_W': _L0_ffn_in['W'], 'L0_ffn_b': _L0_ffn_in['b'], 'L1_gnn_U': _L1_gnn_in['U'], 'L1_gnn_s': _L1_gnn_in['s'], 'L1_gnn_Vt': _L1_gnn_in['Vt'], 'L1_gnn_bias': _L1_gnn_in['bias'], 'L1_mix_w_qkv': _L1_mix_in['w_qkv'], 'L1_mix_w_proj': _L1_mix_in['w_proj'], 'L1_mix_b_proj': _L1_mix_in['b_proj'], 'L1_ffn_fc1_w': _L1_ffn_in['fc1_w'], 'L1_ffn_fc1_b': _L1_ffn_in['fc1_b'], 'L1_ffn_fc2_w': _L1_ffn_in['fc2_w'], 'L1_ffn_fc2_b': _L1_ffn_in['fc2_b']}

def reference(x, src, dst, edge_weight, L0_gnn_W, L0_gnn_b, L0_mix_w_qkv, L0_mix_w_out, L0_mix_b_out, L0_ffn_W, L0_ffn_b, L1_gnn_U, L1_gnn_s, L1_gnn_Vt, L1_gnn_bias, L1_mix_w_qkv, L1_mix_w_proj, L1_mix_b_proj, L1_ffn_fc1_w, L1_ffn_fc1_b, L1_ffn_fc2_w, L1_ffn_fc2_b):
    import jax
    import jax.numpy as jnp

    def _L0_gnn_ref(x, edge_index, edge_attr, W, b):
        import jax, jax.numpy as jnp
        import numpy as np
        N = 1250
        E = 20000
        D_IN = 512
        D_OUT = 512
        n = x.shape[0]
        row, col = (edge_index[0], edge_index[1])
        loop = jnp.arange(n, dtype=edge_index.dtype)
        row_f = jnp.concatenate([row, loop])
        col_f = jnp.concatenate([col, loop])
        ew = jnp.concatenate([edge_attr, jnp.ones((n,), dtype=edge_attr.dtype)])
        deg = jax.ops.segment_sum(ew, col_f, num_segments=n)
        dinv = jnp.where(deg > 0, jax.lax.rsqrt(deg), 0.0)
        norm = dinv[row_f] * ew * dinv[col_f]
        h = x @ W
        msg = h[row_f] * norm[:, None]
        out = jax.ops.segment_sum(msg, col_f, num_segments=n)
        return out + b

    def _L0_mix_ref(x, w_qkv, w_out, b_out):
        import jax, jax.numpy as jnp
        import numpy as np
        DIM = 512
        HEADS = 8
        DIM_HEAD = 64
        INNER = HEADS * DIM_HEAD
        b, n, d = x.shape
        qkv = x @ w_qkv
        q, k, v = jnp.split(qkv, 3, axis=-1)

        def to_heads(t):
            return t.reshape(b, n, HEADS, DIM_HEAD).transpose(0, 2, 1, 3)
        q, k, v = map(to_heads, (q, k, v))
        q = jax.nn.elu(q) + 1.0
        k = jax.nn.elu(k) + 1.0
        kv = jnp.einsum('bhnd,bhnm->bhdm', k, v)
        z = 1.0 / (jnp.einsum('bhnd,bhd->bhn', q, k.sum(axis=2)) + 1e-06)
        out = jnp.einsum('bhnd,bhdm->bhnm', q, kv) * z[..., None]
        out = out.transpose(0, 2, 1, 3).reshape(b, n, INNER)
        return out @ w_out + b_out

    def _L0_ffn_ref(x_bd, W, b):
        import jax, jax.numpy as jnp
        import numpy as np
        MARK_AX = 0
        OP_MUL = 1
        OPCODE_BASE = 2
        ALU_LO, ALU_HI = (64, 80)
        AX_CARRY_LO, AX_CARRY_HI = (96, 112)
        OUTPUT_LO, OUTPUT_HI = (128, 144)
        NIB_A, NIB_B, RESULT, OP_START = (0, 1, 2, 3)
        GE_DIM = 160
        N_POS = 8
        N_LAYERS = 7
        OPCODE = 27

        def _decode_nibble(x16):
            return jnp.argmax(x16 > 0.5, axis=-1).astype(x16.dtype)
        B, S, D = x_bd.shape
        mask = (x_bd[..., MARK_AX] >= 0.5) & (x_bd[..., OP_MUL] >= 0.5)
        a_lo = _decode_nibble(x_bd[..., ALU_LO:ALU_LO + 16])
        a_hi = _decode_nibble(x_bd[..., ALU_HI:ALU_HI + 16])
        b_lo = _decode_nibble(x_bd[..., AX_CARRY_LO:AX_CARRY_LO + 16])
        b_hi = _decode_nibble(x_bd[..., AX_CARRY_HI:AX_CARRY_HI + 16])
        op_val = x_bd[..., OPCODE_BASE + OPCODE]
        x_ge = jnp.zeros((B, S, N_POS, GE_DIM), dtype=x_bd.dtype)
        x_ge = x_ge.at[..., 0, NIB_A].set(a_lo)
        x_ge = x_ge.at[..., 1, NIB_A].set(a_hi)
        x_ge = x_ge.at[..., 0, NIB_B].set(b_lo)
        x_ge = x_ge.at[..., 1, NIB_B].set(b_hi)
        x_ge = x_ge.at[..., :, OP_START + OPCODE].set(op_val[..., None])
        h = x_ge
        for i in range(N_LAYERS):
            h = jnp.einsum('bspd,ed->bspe', h, W[i]) + b[i]
            if i < N_LAYERS - 1:
                h = jax.nn.relu(h)
        res_lo = jnp.clip(jnp.round(h[..., 0, RESULT]), 0, 15).astype(jnp.int32)
        res_hi = jnp.clip(jnp.round(h[..., 1, RESULT]), 0, 15).astype(jnp.int32)
        m = mask[..., None].astype(x_bd.dtype)
        add_lo = 2.0 * jax.nn.one_hot(res_lo, 16, dtype=x_bd.dtype) * m
        add_hi = 2.0 * jax.nn.one_hot(res_hi, 16, dtype=x_bd.dtype) * m
        out = x_bd.at[..., OUTPUT_LO:OUTPUT_LO + 16].add(add_lo)
        out = out.at[..., OUTPUT_HI:OUTPUT_HI + 16].add(add_hi)
        return out

    def _L1_gnn_ref(input, U, s, Vt, bias, edge_row, edge_col, edge_val):
        import jax, jax.numpy as jnp
        import numpy as np
        N_NODES = 12500
        N_EDGES = 400000
        IN_F = 512
        OUT_F = 512
        RANK = 64
        support = input @ U * s
        support = support @ Vt
        gathered = support[edge_col] * edge_val[:, None]
        output = jax.ops.segment_sum(gathered, edge_row, num_segments=input.shape[0])
        output = output + bias
        return jax.nn.relu(output)

    def _L1_mix_ref(x, w_qkv, w_proj, b_proj):
        import jax, jax.numpy as jnp
        import numpy as np
        NUM_HEADS = 8
        B, N, C = x.shape
        H = NUM_HEADS
        D = C // H
        qkv = (x @ w_qkv).reshape(B, N, 3, H, D)
        qkv = jnp.transpose(qkv, (2, 0, 3, 1, 4))
        q, k, v = (qkv[0], qkv[1], qkv[2])
        q = jax.nn.softmax(q, axis=-1)
        k = jax.nn.softmax(jax.nn.elu(k) + 1.0, axis=-2)
        context = jnp.einsum('bhnd,bhne->bhde', k, v)
        out = jnp.einsum('bhnd,bhde->bhne', q, context)
        out = jnp.transpose(out, (0, 2, 1, 3)).reshape(B, N, C)
        return out @ w_proj + b_proj

    def _L1_ffn_ref(x, fc1_w, fc1_b, fc2_w, fc2_b):
        import jax, jax.numpy as jnp
        import numpy as np

        def _haar_dwt2(x):
            a = x[:, ::2, ::2]
            b = x[:, ::2, 1::2]
            c = x[:, 1::2, ::2]
            d = x[:, 1::2, 1::2]
            ll = (a + b + c + d) * 0.5
            lh = (a + b - c - d) * 0.5
            hl = (a - b + c - d) * 0.5
            hh = (a - b - c + d) * 0.5
            return (ll, lh, hl, hh)

        def _haar_idwt2(ll, lh, hl, hh):
            a = (ll + lh + hl + hh) * 0.5
            b = (ll + lh - hl - hh) * 0.5
            c = (ll - lh + hl - hh) * 0.5
            d = (ll - lh - hl + hh) * 0.5
            B, H2, W2 = ll.shape
            out = jnp.zeros((B, 2 * H2, 2 * W2), ll.dtype)
            out = out.at[:, ::2, ::2].set(a)
            out = out.at[:, ::2, 1::2].set(b)
            out = out.at[:, 1::2, ::2].set(c)
            out = out.at[:, 1::2, 1::2].set(d)
            return out

        def _interp_linear_last(x, m):
            n = x.shape[-1]
            pos = jnp.linspace(0.0, 1.0, m, dtype=x.dtype) * (n - 1)
            i0 = jnp.clip(jnp.floor(pos).astype(jnp.int32), 0, n - 2)
            w = pos - i0.astype(x.dtype)
            return x[..., i0] * (1.0 - w) + x[..., i0 + 1] * w
        b, f, c = x.shape
        ll, lh, hl, hh = _haar_dwt2(x)
        ll_up = _interp_linear_last(ll, c)
        h = jax.nn.gelu(jnp.einsum('bfc,hc->bfh', ll_up, fc1_w) + fc1_b, approximate=False)
        ll_new = jnp.einsum('bfh,oh->bfo', h, fc2_w) + fc2_b
        return _haar_idwt2(ll_new, lh, hl, hh)
    edge_index = jnp.stack([src, dst])
    xn = _layernorm(x, axis=-1)
    x = x + _L0_gnn_ref(xn, edge_index, edge_weight, L0_gnn_W, L0_gnn_b) + _L0_mix_ref(xn[None], L0_mix_w_qkv, L0_mix_w_out, L0_mix_b_out)[0]
    x = x + _L0_ffn_ref(_layernorm(x, axis=-1)[None], L0_ffn_W, L0_ffn_b)[0]
    xn = _layernorm(x, axis=-1)
    x = x + _L1_gnn_ref(xn, L1_gnn_U, L1_gnn_s, L1_gnn_Vt, L1_gnn_bias, src, dst, edge_weight) + _L1_mix_ref(xn[None], L1_mix_w_qkv, L1_mix_w_proj, L1_mix_b_proj)[0]
    x = x + _L1_ffn_ref(_layernorm(x, axis=-1)[None], L1_ffn_fc1_w, L1_ffn_fc1_b, L1_ffn_fc2_w, L1_ffn_fc2_b)[0]
    return x

_drawn_inputs = setup_inputs


def setup_inputs(seed=0):
    import zlib

    import numpy as np

    out = dict(_drawn_inputs(seed))
    spreads = {'L1_mix_b_proj': (0.0, 0.1), 'L1_ffn_fc1_b': (0.0, 0.8), 'L1_ffn_fc2_b': (0.0, 0.473)}
    factors = {'L0_mix_b_out': 3.92, 'L1_gnn_bias': 8.0, 'L1_ffn_fc1_w': 4.971, 'L1_ffn_fc2_w': 4.323}
    for name, (base, spread) in spreads.items():
        noise = np.random.default_rng([zlib.crc32(name.encode()), seed]).standard_normal(out[name].shape)
        drawn = base * np.exp(spread * noise) if base else spread * noise
        out[name] = jnp.asarray(drawn.astype(out[name].dtype))
    for name, factor in factors.items():
        out[name] = (out[name] * factor).astype(out[name].dtype)
    return out
```

```python
from contextlib import ExitStack

import numpy as np

import concourse.bass as bass
from concourse import mybir

F32 = mybir.dt.float32
F32R = mybir.dt.float32r
I32 = mybir.dt.int32
ALU = mybir.AluOpType
ACT = mybir.ActivationFunctionType
AX = mybir.AxisListType.X

P = 128
N, D, E = 1250, 512, 21250
T = -(-N // P)
NP = T * P
LAST = N - (T - 1) * P
KC = D // P
HEADS, DH = 8, 64
PAIRS = HEADS // 2
VC = P + 2
EPS = 1e-5
CH = 170
CP = CH // 2
WIN = 20
ITER = T // 2
CPI = CP // ITER
RANK = 64
GE = 160
DEG_DVE = 6
ROUND = 12582912.0
FFL = 7
HALF = D // 2
REM = GE - P
FX = 3 * REM + 2
FM = P + 3 * REM
FK = P + FX
FC = T // 2
FN = 2 * P
STEPS = FFL * FC


def interpolation():
    step = np.arange(D, dtype=np.float32) * np.float32(1 / (D - 1))
    pos = step * np.float32(HALF - 1)
    i0 = np.clip(np.floor(pos).astype(np.int64), 0, HALF - 2)
    w = pos - i0.astype(np.float32)
    m = np.zeros((D, HALF), np.float32)
    m[np.arange(D), i0] = np.float32(1) - w
    m[np.arange(D), i0 + 1] += w
    return m


def ds(a, n):
    return bass.ds(a, n)


def later(t, n):
    return not isinstance(t, int) or t >= n


def row(x, t):
    return x[:, ds(t, 1), :].rearrange("p a n -> p (a n)")


def build(nc, a, out):
    ctx = ExitStack()
    with ctx:
        def sb(name, shape, dt=F32, at=ctx):
            return at.enter_context(nc.sbuf_tensor(name, shape, dt))

        def sem(name):
            return ctx.enter_context(nc.semaphore(name))

        nodes = sb("nodes", [P, T, D])
        xn = sb("xn", [P, 2, D])
        et = sb("et", [P, D])
        rt = sb("rt", [P, D])
        ident = sb("ident", [P, P])
        onesf = sb("onesf", [P, P])
        ones2 = sb("ones2", [P, 2], F32R)
        stat = sb("stat", [P, T, 6])
        mv = sb("mv", [P, T, 2])
        rstd = sb("rstd", [P, T])
        nmr = sb("nmr", [P, T])
        outside = sb("outside", [P, 1])
        baserow = sb("baserow", [1, CP])
        baseint = sb("baseint", [1, CP], I32)
        flagint = sb("flagint", [1, 1], I32)
        ksum = sb("ksum", [P, PAIRS])

        def region(name, *groups):
            made, size = {}, 0
            for group in groups:
                used = 0
                with ExitStack() as r:
                    for n, shape, *dt in group:
                        made[n] = sb(n, shape, *(dt or [F32]), r)
                        used += -(-4 * int(np.prod(shape[1:])) // 32) * 32
                size = max(size, used)
            sb(name, [P, size // 4])
            return made

        RQ = region("hold_qbuf",
                    [("qbuf", [P, T, D])],
                    [("N1", [P, FFL, FK]), ("N2", [P, FFL - 1, FK])])
        qbuf, N1, N2 = (RQ[n] for n in ("qbuf", "N1", "N2"))
        RE = region("hold_edges",
                    [("srclo", [P, CH]), ("key", [P, CH]), ("whl", [P, CH, 2], F32R),
                     ("iota_src", [P, P]), ("iota_key", [P, T * WIN]),
                     ("rest", [P, 3, CH])],
                    [("N0", [P, 2, 2, 20]), ("hin", [P, FFL, REM + 1], F32R), ("st3", [P, T, 3, 6]),
                     ("pairs", [P, P]), ("rows1", [2, 2, P], F32R),
                     ("wt16", [P, 4, 16]), ("iota16", [P, 16]), ("pairm", [P, P], F32R),
                     ("pairq", [P, DH], F32R), ("hif", [P, T, 6], F32R), ("sumq", [P, T, HEADS]),
                     ("w3", [P, 2, 4]), ("w3h", [P, 2, 4], F32R), ("w3l", [P, 2, 4]), ("mask2", [P, T]),
                     ("res", [P, T, 2]), ("nmr2", [P, T])])
        srclo, key, whl, iota_src, iota_key = (RE[n] for n in ("srclo", "key", "whl", "iota_src", "iota_key"))
        rest = RE["rest"]
        wt16, iota16, pairm, pairq, hif, sumq, w3 = (RE[n] for n in ("wt16", "iota16", "pairm", "pairq", "hif", "sumq", "w3"))
        w3h, w3l, mask2, res, nmr2 = (RE[n] for n in ("w3h", "w3l", "mask2", "res", "nmr2"))
        N0, hin, st3, pairs, rows1 = (RE[n] for n in ("N0", "hin", "st3", "pairs", "rows1"))
        RA = region("hold_AT",
                    [("AT", [P, T, NP])],
                    [("sn", [P, T, HALF]), ("llT", [P, 2, 2, NP // 2], F32R), ("hf", [P, 2, NP // 2]),
                     ("hT", [P, 2, 2, NP], F32R)])
        AT, sn, llT, hf, hT = (RA[n] for n in ("AT", "sn", "llT", "hf", "hT"))
        R0 = region("hold_xT",
                    [("xT", [P, 2, 2, KC, P], F32R)],
                    [("X128", [P, T, P]), ("F20", [P, T, 20]), ("F6", [P, T, 6]), ("first", [P, T, 4]),
                     ("oneh", [P, T, 32])])
        xT, X128, F20, F6, first1, oneh = (R0[n] for n in ("xT", "X128", "F20", "F6", "first", "oneh"))
        R1 = region("hold_raw",
                    [("erow", [P, 3, 2, P], I32), ("frow", [P, 4, 2, P], F32)],
                    [("edge", [P, 4, CH]), ("onehot", [P, 3, 2, P]), ("away", [P, 3, T * WIN])],
                    [("raw", [P, KC, D], F32)],
                    [("xb", [P, 2, D]), ("brow", [P, 2, D])],
                    [("vraw", [P, D]), ("agT", [P, 2, 2, P], F32R), ("b2", [P, 2, D], F32R)])
        erow, frow, edge, raw, xb, brow = (R1[n] for n in ("erow", "frow", "edge", "raw", "xb", "brow"))
        onehot_, away = R1["onehot"], R1["away"]
        vraw, agT, b2 = (R1[n] for n in ("vraw", "agT", "b2"))
        R2 = region("hold_weights",
                    [("wraw", [P, 4, 2, KC, D])],
                    [("wsl", [P, 4, 2, KC, D], F32R)],
                    [("degp", [P, 2, NP]), ("dhl", [P, 2, NP], F32R)],
                    [("G", [P, 2, T, D], F32R), ("ggap", [P, 4 * D]), ("WO", [P, 2, KC, D], F32R)],
                    [("H", [P, 2, FC, 2 * FN], F32R), ("Rr", [P, FC, 2 * FN], F32R),
                     ("FWm", [P, 2, FFL - 2, FM], F32R), ("FWx", [P, FFL - 2, FM], F32R),
                     ("FW0", [P, 2, FM], F32R), ("w6", [P, 4], F32R), ("w6x", [P, 2], F32R),
                     ("FT", [P, NP], F32R)],
                    [("kbuf", [P, T, D]), ("Wq", [P, 2, KC, D], F32R), ("Wu", [P, 2, KC, RANK], F32R),
                     ("uhl", [P, T, 2 * RANK], F32R), ("kmax", [P, D]), ("kmaxb", [P, D]), ("Wk", [P, 2, KC, D], F32R)],
                    [("ZT", [P, 2, KC, D], F32R), ("zgap", [P, D * 2]), ("Wp", [P, 2, KC, D], F32R),
                     ("ugap", [P, 2 * KC * RANK + T * 2 * RANK]), ("Vt", [P, 2, D], F32R), ("khl2", [P, 2, 2, D], F32R)],
                    [("PTr", [P, KC, HALF]), ("PTh", [P, 2, KC, HALF], F32R), ("f1r", [P, 2, D]),
                     ("f1T", [P, 2, KC, HALF], F32R), ("f2r", [P, 2, HALF]), ("f2T", [P, 2, 2, HALF], F32R),
                     ("W1", [P, 2, 2, HALF], F32R), ("b3r", [P, HALF]), ("b3", [P, HALF], F32R),
                     ("vgap", [P, 2 * KC * RANK + T * 2 * RANK + 2 * D]), ("MW", [P, 2, KC, D], F32R)])
        wraw, dhl = R2["wraw"], R2["dhl"]
        wsl, G, degp, WO = (R2[n] for n in ("wsl", "G", "degp", "WO"))
        H, Rr, FWm, FWx, FW0, w6, w6x, FT = (R2[n] for n in ("H", "Rr", "FWm", "FWx", "FW0", "w6", "w6x", "FT"))
        kbuf, Wq, Wu, uhl, kmax, kmaxb, Wk = (R2[n] for n in ("kbuf", "Wq", "Wu", "uhl", "kmax", "kmaxb", "Wk"))
        ZT, Wp, Vt, khl2, MW = (R2[n] for n in ("ZT", "Wp", "Vt", "khl2", "MW"))
        PTr, PTh, f1r, f1T, f2r, f2T, W1, b3r, b3 = (R2[n] for n in ("PTr", "PTh", "f1r", "f1T", "f2r", "f2T", "W1", "b3r", "b3"))
        R3 = region("hold_scratch",
                    [("khl", [P, 2, D], F32R), ("vhl", [P, 2, PAIRS, VC], F32R),
                     ("Loh", [P, 3, 2, 2, P], F32R), ("Roh", [P, 3, 2, T * WIN], F32R)],
                    [("ATs", [P, 2, 2, T, P], F32R)],
                    [("Wv", [P, 2, KC, D], F32R), ("qx", [P, 2, D])],
                    [("shl", [P, 2, T, HALF], F32R)])
        khl, vhl, Loh, Roh, ATs, Wv, qx, shl = (R3[n] for n in ("khl", "vhl", "Loh", "Roh", "ATs", "Wv", "qx", "shl"))

        def pb(name):
            return ctx.enter_context(nc.psum_tensor(name, [P, 512], F32))

        pT, pQ, pK, pV, pH, pA = (pb(n) for n in ("pT", "pQ", "pK", "pV", "pH", "pA"))
        pKV = [pb("pKV0"), pb("pKV1")]
        pG, pM = (pK, pV), (pH, pQ)
        fmain, frest = (pK, pV, pH), (pQ, pA, pKV[1])
        wbank = (pT, pKV[0], pA, pKV[1], pH, pT, pKV[0])
        mbank = (pH, pQ, pKV[0], pKV[1])
        obank = (pKV[0], pKV[1], pK, pV)

        def chunk_bank(u, c):
            return (pA, pKV[1])[(u + c) % 2]


        deg = sb("deg", [P, T])
        dinv = sb("dinv", [P, T])
        dinv2 = sb("dinv2", [P, T])
        small = sb("small", [P, 4, T])
        den = sb("den", [P, HEADS])

        s2 = sb("s2", [P, 1])
        fb1 = sb("fb1", [P, 2])
        lomask = sb("lomask", [P, 1])

        S = {}

        def s(name):
            if name not in S:
                S[name] = sem(name)
            return S[name]

        for n in ("ld_edge", "ld_x", "ld_x2", "ld_w0", "ld_w1", "ld_w2", "ld_w3", "ld_wo",
                  "c_pool", "c_dve", "w_hi", "w_lo", "w_lo2", "ld_xb", "e_dve", "e_pe", "sd",
                  "at_zero", "consts", "pad_zero", 
                  "xn_ok", "xt_ps", "xt_hi", "xt_lo", "q_mm", "k_mm", "v_mm", "h_mm", "kv_mm",
                  "q_er", "q_elu", "k_er", "k_elu", "k_hi", "k_lo", "v_hi", "v_lo", "h_out",
                  "oh_dve", "rest_ok", "rest_ps", "flag_ok", "rs", "rest_oh", "rest_mm", "rest_acc", "oh_act", "oh_src", "oh_pool", "oh_y", "a_mm", "a_acc", "out_st",
                  "bd_ok", "degp_ok", "degp_pool", "at_done", "dhl_hi", "dhl_lo", "kvt_ps", "ksb_ps", "deg_ps", "deg_ok", "deg_sqrt", "dinv_ok",
                  "g_hi", "g_lo", "wo_hi", "wo_lo", "kvt_hi", "kvt_lo", "ksb_ok", "m_mm", "m_hi", "m_lo",
                  "ats_hi", "ats_lo", "agg_mm", "mix_mm", "qs_ok", "qt_ps", "qt_hi", "qt_lo", "x_ld0", "x_ld1", "b_ld",
                  "xb_ok", "x1_ok", "bias_ok",
                  "ln_var", "ln_sqrt", "ln_ok", "x128_ok", "y_ok", "fw_ld", "fp", "fn_ok", "pads_ok", "f20_ok",
                  "fw_ps", "fw_hi", "fw_lo", "ft_ps", "ft_ok", "f_mm", "f_hi", "f_lo", "f6_mm", "x2_ok",
                  "init2", "z_xlo", "ld_small",
                  "v1_hi", "v1_lo", "p1_lo", "kmax_z", "kmax_ok", "sq", "c1", "zs_a", "zs_d", "kz", "kt_lo", "vt_lo", "b2_ok", "a2_ps", "a2_lo", "sx", "pt_lo", "b3_ok",
                  "f1_ps", "f1_hi", "f1_lo", "f2_ps", "f2_hi", "f2_lo", "w1_mm", "w1_hi", "w1_lo",
                  "s_add", "s_n", "s_hi", "s_lo", "ll_mm", "ll_hi", "ll_lo", "hh_mm", "hh_g", "hh_hi", "hh_lo", "o_mm", "o_ok"):
            s(n)

        after = {}
        for name, first_name, count in (
                ("k1_hi", "v1_hi", 1), ("p1_hi", "k1_hi", 1), ("pt_hi", "p1_hi", KC), ("k1_lo", "v1_lo", 1), ("q1_lo", "k1_lo", 1), ("u1_lo", "q1_lo", 1),
                ("n_xn", "xn_ok", T), ("z_xn", "n_xn", T), ("n_hi", "xt_hi", T), ("z_xhi", "n_hi", T),
                ("nk_er", "q_er", 2 * T), ("nq_exp", "k_er", 2 * T), ("z_khi", "k_hi", T), ("z_exp", "v_hi", T),
                ("nu_hi", "h_out", T), ("q1_hi", "w_hi", 4), ("u1_hi", "wo_hi", 1), ("zt_hi", "kvt_hi", 1),
                ("cmb_ok", "ksb_ok", 1), ("mw_hi", "m_hi", 4), ("kt_hi", "g_hi", T), ("a2_hi", "ats_hi", T),
                ("r2_hi", "qt_hi", T), ("g2_hi", "fw_hi", FFL), ("vt_hi", "ft_ok", 3), ("n_ps", "xt_ps", T),
                ("nq_mm", "q_mm", T), ("nk_mm", "k_mm", T), ("nu_mm", "v_mm", T), ("z_mm", "kv_mm", T),
                ("cmb_ps", "ksb_ps", 1), ("cm_ps", "kvt_ps", 1), ("zt_ps", "cm_ps", 1), ("mw_mm", "m_mm", 4),
                ("a2_mm", "agg_mm", T), ("m2_mm", "mix_mm", T), ("r2_ps", "qt_ps", T), ("s2_mm", "h_mm", T),
                ("kt_mm", "deg_ps", 1), ("n_lo", "xt_lo", T), ("nq_sub", "q_elu", T), ("nk_elu", "k_elu", T),
                ("nu_lo", "v_lo", T), ("cm_ok", "bd_ok", 1), ("zt_lo", "kvt_lo", 1), ("mw_lo", "m_lo", 4),
                ("z_klo", "g_lo", T), ("z_sub", "qs_ok", T), ("r2_lo", "qt_lo", T), ("r2_qs", "z_sub", T),
                ("x3_ok", "x1_ok", T), ("zr_ok", "degp_ok", 2), ("g2_lo", "fw_lo", FFL - 1),
                ("y2_ok", "y_ok", T), ("ld_q1", "ld_w0", 16), ("ld_k1", "ld_w1", 16), ("ld_u1", "ld_w2", 16),
                ("ld_v1", "ld_w3", 16), ("ld_wp", "ld_wo", 16), ("ld_v2", "ld_x", 16), ("ld_b2", "b_ld", 32),
                ("ld_f1", "ld_edge", 16 * 9)):
            S[name] = S[first_name]
            after[name] = after.get(first_name, 0) + count

        w4 = [a["L0_mix_w_qkv"][:, 0:D], a["L0_mix_w_qkv"][:, D:2 * D], a["L0_mix_w_qkv"][:, 2 * D:3 * D], a["L0_gnn_W"]]
        block = ctx.enter_context(nc.Block())

        def pairs_by(products, first):
            return (products * CPI) // 8 if not first else max(0, (products - 4) * CPI // 4)

        def slot_free(eng, g, j, first):
            back = 3 if j >= 3 else (2, 2, 5)[j]
            if not (first and j < 3):
                eng.wait_ge(S["a_mm"], g - back + 1)

        def wview(w):
            return w.rearrange("(c p) n -> p c n", p=P)

        @block.sync
        def _(sp):
            sp.wait_ge(S["pad_zero"], 1)
            full = (E // P) // P * P * P
            rows2 = E // P - P
            tail = E - (E // P) * P
            for k, name in enumerate(("src", "dst", "edge_weight")):
                v = a[name] if name != "edge_weight" else a[name].bitcast(I32)
                sp.dma_start(erow[:, k, 0, :], v[0:full].rearrange("(c p) -> c p", p=P)).then_inc(S["ld_edge"], 16)
                sp.dma_start(erow[0:rows2, k, 1, :], v[full:full + rows2 * P].rearrange("(c p) -> c p", p=P)).then_inc(S["ld_edge"], 16)
                sp.dma_start(erow[rows2:rows2 + 1, k, 1, 0:tail], v[E - tail:E].rearrange("(a p) -> a p", a=1)).then_inc(S["ld_edge"], 16)
            sp.wait_ge(S["pad_zero"], 2)
            sp.dma_start(nodes[0:LAST, T - 1, :], a["x"][(T - 1) * P:N, :]).then_inc(S["ld_x2"], 16)
            sp.wait_ge(S["ld_x"], 16)
            sp.dma_start(wraw[:, 1, 1], wview(w4[1])).then_inc(S["ld_w1"], 16)
            sp.dma_start(wraw[:, 2, 1], wview(w4[2])).then_inc(S["ld_w2"], 16)
            sp.dma_start(wraw[:, 3, 1], wview(w4[3])).then_inc(S["ld_w3"], 16)
            sp.wait_ge(S["oh_pool"], CP)
            sp.wait_ge(S["oh_act"], CP)
            sp.dma_start(raw[:], wview(a["L0_mix_w_out"])).then_inc(S["ld_wo"], 16)

            sp.wait_ge(S["wo_lo"], 1)
            for k, name in enumerate(("L0_gnn_b", "L0_mix_b_out")):
                sp.dma_start(brow[:, k, :], a[name].partition_broadcast(P)).then_inc(S["b_ld"], 16)

            def x_again(t, u, rows=P, first=False):
                if not first:
                    sp.wait_ge(S["x1_ok"], t - 1)
                src = a["x"][ds(t * P, rows), :]
                sp.dma_start(xb[0:rows, u, :], src).then_inc(S[f"x_ld{u}"], 16)

            x_again(0, 0, first=True)
            x_again(1, 1, first=True)
            with sp.Fori(1, ITER - 1) as i:
                x_again(2 * i, 0)
                x_again(2 * i + 1, 1)
            sp.wait_ge(S["qs_ok"], 6)
            W, b = a["L0_ffn_W"], a["L0_ffn_b"]
            sp.dma_start(N1[:, :, 0:GE], W[:, 0:P, :].rearrange("l e d -> e l d")).then_inc(S["fw_ld"], 16)
            for r in range(3):
                sp.dma_start(N2[r * REM:(r + 1) * REM, :, 0:GE], W[0:FFL - 1, P:GE, :].rearrange("l e d -> e l d")).then_inc(S["fw_ld"], 16)
            with nc.allow_non_contiguous_dma(reason="columns of weights and biases"):
                sp.dma_start(N1[:, :, P + 3 * REM:P + 3 * REM + 1], b[:, 0:P].rearrange("l (e a) -> e l a", a=1)).then_inc(S["fw_ld"], 16)
                for r in range(3):
                    rows = slice(r * REM, (r + 1) * REM)
                    sp.dma_start(N2[rows, :, P + 3 * REM:P + 3 * REM + 1], b[0:FFL - 1, P:GE].rearrange("l (e a) -> e l a", a=1)).then_inc(S["fw_ld"], 16)

            x_again(T - 2, 0)
            x_again(T - 1, 1, LAST)


            with nc.allow_non_contiguous_dma(reason="vectors across partitions"):
                for h in range(2):
                    sp.dma_start(s2[h * RANK:(h + 1) * RANK, :], a["L1_gnn_s"].rearrange("(r a) -> r a", a=1)).then_inc(S["ld_small"], 16)
                sp.dma_start(fb1[:], a["L1_ffn_fc1_b"].rearrange("(b p) -> p b", p=P)).then_inc(S["ld_small"], 16)
            w1 = [a["L1_mix_w_qkv"][:, k * D:(k + 1) * D] for k in range(3)]
            sp.wait_ge(S["x1_ok"], T)
            sp.dma_start(raw[:], wview(w1[2])).then_inc(S["ld_v1"], 16)
            sp.wait_ge(S["fw_ps"], FFL)
            sp.dma_start(qbuf[:, 4:8, :], wview(w1[1])).then_inc(S["ld_k1"], 16)
            sp.dma_start(qbuf[:, 0:4, :], wview(w1[0])).then_inc(S["ld_q1"], 16)
            sp.dma_start(qbuf[:, 8, 0:KC * RANK].rearrange("p (c n) -> p c n", c=KC), wview(a["L1_gnn_U"])).then_inc(S["ld_u1"], 16)
            sp.wait_ge(S["v1_lo"], 1)
            sp.dma_start(raw[:], wview(a["L1_mix_w_proj"])).then_inc(S["ld_wp"], 16)
            sp.wait_ge(S["p1_lo"], KC)
            for h in range(2):
                sp.dma_start(vraw[h * RANK:(h + 1) * RANK, :], a["L1_gnn_Vt"][:, :]).then_inc(S["ld_v2"], 16)
            sp.wait_ge(S["zt_ps"], 1 + after["zt_ps"])
            for k, name in enumerate(("L1_gnn_bias", "L1_mix_b_proj")):
                sp.dma_start(xn[0:2, k, :], a[name].partition_broadcast(2)).then_inc(S["ld_b2"], 16)
            sp.wait_ge(S["mw_mm"], PAIRS + after["mw_mm"])
            sp.dma_start(PTr[:], a["interp"].rearrange("(c p) n -> p c n", p=P)).then_inc(S["ld_f1"], 16)
            sp.dma_start(f1r[:], a["L1_ffn_fc1_w"].rearrange("(b p) n -> p b n", p=P)).then_inc(S["ld_f1"], 16)
            sp.dma_start(f2r[:], a["L1_ffn_fc2_w"].rearrange("(b p) n -> p b n", p=P)).then_inc(S["ld_f1"], 16)
            sp.dma_start(b3r[0:2, :], a["L1_ffn_fc2_b"].partition_broadcast(2)).then_inc(S["ld_f1"], 16)

            for t in range(T):
                rows = LAST if t == T - 1 else P
                sp.wait_ge(S["o_ok"], t + 1)
                sp.dma_start(out[t * P:t * P + rows, :], nodes[0:rows, t, :]).then_inc(S["out_st"], 16)
            sp.wait_ge(S["out_st"], 16 * T)

        @block.scalar
        def _(act):
            for name, t0, t1 in (("ld_x", 0, 5), ("ld_xb", 5, T - 1)):
                act.dma_start(nodes[:, t0:t1, :], a["x"][t0 * P:t1 * P, :].rearrange("(t p) n -> p t n", p=P)).then_inc(S[name], 16)
            act.dma_start(wraw[:, 0, 1], wview(w4[0])).then_inc(S["ld_w0"], 16)
            def ln_sqrt(n):
                act.wait_ge(S["ln_var"], n)
                act.activation(rstd[:], small[:, 3, :], ACT.Sqrt).then_inc(S["ln_sqrt"], 1)

            def split_hi(i):
                act.wait_ge(S[f"ld_w{i}"], 16)
                act.activation(wsl[:, i, 0], wraw[:, i, 1], ACT.Copy).then_inc(S["w_hi"], 1)

            split_hi(0)
            split_hi(1)
            ln_sqrt(1)

            def normalise(t, u):
                if later(t, 2):
                    act.wait_ge(S["xt_ps"], t - 1)
                act.activation(xn[:, u, :], nodes[:, ds(t, 1), :].rearrange("p a n -> p (a n)"), ACT.Identity,
                               bias=nmr[:, ds(t, 1)], scale=rstd[:, ds(t, 1)]).then_inc(S["xn_ok"], 1)

            def xt_hi(t, u):
                act.wait_ge(S["xt_ps"], t + 1)
                if later(t, 2):
                    act.wait_ge(S["h_mm"], t - 1)
                act.activation(xT[:, u, 0, :, :], pT[:, :].rearrange("p (c n) -> p c n", c=KC), ACT.Copy).then_inc(S["xt_hi"], 1)

            act.wait_ge(S["ln_ok"], 1)
            normalise(0, 0)
            normalise(1, 1)
            xt_hi(0, 0)
            split_hi(2)
            split_hi(3)

            def onehot(g, j, first):
                slot_free(act, g, j, first)
                act.activation(away[:, j % 3, :], iota_key[:], ACT.Abs, bias=key[:, ds(2 * g, 1)], scale=-1.0).then_inc(S["oh_y"], 1)
                act.wait_ge(S["oh_y"], g + 1)
                act.activation(Roh[:, j % 3, 0, :], away[:, j % 3, :], ACT.Relu, bias=onesf[:, 0:1], scale=-1.0).then_inc(S["oh_act"], 1)

            made = [0]

            def onehots_upto(i, n, first):
                while made[0] < min(n, CPI):
                    if first and made[0] == 0:
                        act.wait_ge(S["e_dve"], 1)
                    onehot(CPI * i + made[0], made[0], first)
                    made[0] += 1

            def tile(t, u, nxt, nxt2, i=None, first=False):
                def ahead(k):
                    if not first or 4 * u + k >= 3:
                        onehots_upto(i, pairs_by(4 * u + k + 1, first) + 2, first)
                ahead(0)
                act.wait_ge(S["q_mm"], t + 1)
                if later(t, 1):
                    act.wait_ge(S["k_elu"], t)
                act.activation(et[:], pQ[:, :], ACT.Exp).then_inc(S["q_er"], 1)
                qv = qbuf[:, ds(t, 1), :].rearrange("p a n -> p (a n)")
                act.activation(qv, pQ[:, :], ACT.Relu).then_inc(S["q_er"], 1)
                ahead(1)
                act.wait_ge(S["k_mm"], t + 1)
                act.wait_ge(S["q_elu"], t + 1)
                if later(t, 1):
                    act.wait_ge(S["k_lo"], t)
                act.activation(et[:], pK[:, :], ACT.Exp).then_inc(S["k_er"], 1)
                act.activation(rt[:], pK[:, :], ACT.Relu).then_inc(S["k_er"], 1)
                act.wait_ge(S["k_elu"], t + 1)
                if later(t, 1):
                    act.wait_ge(S["kv_mm"], t)
                act.activation(khl[:, 0, :], rt[:], ACT.Copy).then_inc(S["k_hi"], 1)
                ahead(2)
                act.wait_ge(S["v_mm"], t + 1)
                act.activation(vhl[:, 0, :, 0:P], pV[:, :].rearrange("p (c n) -> p c n", c=PAIRS), ACT.Copy).then_inc(S["v_hi"], 1)
                if nxt:
                    xt_hi(t + 1, 1 - u)
                if nxt2:
                    normalise(t + 2, u)
                ahead(3)
                act.wait_ge(S["h_mm"], t + 1)
                act.activation(nodes[:, ds(t, 1), :].rearrange("p a n -> p (a n)"), pH[:, :], ACT.Copy).then_inc(S["h_out"], 1)

            tile(0, 0, True, True, 0, True)
            tile(1, 1, True, True, 0, True)
            with act.Fori(1, ITER - 1) as i:
                made[0] = 0
                tile(2 * i, 0, True, True, i)
                tile(2 * i + 1, 1, True, True, i)
            made[0] = 0
            tile(T - 2, 0, True, False, ITER - 1)
            tile(T - 1, 1, False, False, ITER - 1)

            def ats_hi(t, u, first=False):
                if not first:
                    act.wait_ge(S["agg_mm"], t - 1)
                act.activation(ATs[:, u, 0], AT[:, :, ds(t * P, P)], ACT.Copy).then_inc(S["ats_hi"], 1)

            act.wait_ge(S["at_done"], 1)
            act.wait_ge(S["kv_mm"], T)
            ats_hi(0, 0, True)
            act.wait_ge(S["degp_ok"], 2)
            act.activation(dhl[:, 0, :], degp[:, 0, :], ACT.Copy).then_inc(S["dhl_hi"], 1)
            act.wait_ge(S["ld_wo"], 16)
            act.activation(WO[:, 0], raw[:], ACT.Copy).then_inc(S["wo_hi"], 1)
            act.wait_ge(S["kvt_ps"], 1)
            act.activation(xT[:, 0, 0], pT[:, :].rearrange("p (c n) -> p c n", c=KC), ACT.Copy).then_inc(S["kvt_hi"], 1)
            act.wait_ge(S["ksb_ps"], 1)
            act.activation(xn[:, 0, :], pQ[:, :], ACT.Copy).then_inc(S["ksb_ok"], 1)
            ats_hi(1, 1, True)
            act.wait_ge(S["deg_ok"], 1)
            act.activation(dinv[:], small[:, 0, :], ACT.Sqrt).then_inc(S["deg_sqrt"], 1)
            act.wait_ge(S["dinv_ok"], 1)
            for t in range(T):
                act.activation(G[:, 0, t, :], nodes[:, t, :], ACT.Copy, scale=dinv[:, t:t + 1]).then_inc(S["g_hi"], 1)
            for p, bank in enumerate(mbank):
                act.wait_ge(S["m_mm"], p + 1)
                act.activation(WO[:, 0, p, :], bank[:, :], ACT.Copy).then_inc(S["m_hi"], 1)

            def qt_hi(t, u, first=False):
                act.wait_ge(S["qt_ps"], t + 1)
                if not first:
                    act.wait_ge(S["mix_mm"], t - 1)
                act.activation(xT[:, u, 0], pT[:, :].rearrange("p (c n) -> p c n", c=KC), ACT.Copy).then_inc(S["qt_hi"], 1)

            qt_hi(0, 0, True)
            qt_hi(1, 1, True)
            with act.Fori(1, ITER) as i:
                for u in range(2):
                    ats_hi(2 * i + u, u)
                    qt_hi(2 * i + u, u)

            ln_sqrt(2)
            for l in range(FFL):
                bank = wbank[l]
                act.wait_ge(S["fw_ps"], l + 1)
                if l == 0:
                    for pos in range(2):
                        ins = act.activation(FW0[0:20, pos, :], bank[0:20, pos * FM:(pos + 1) * FM], ACT.Copy)
                elif l < FFL - 1:
                    act.activation(FWm[:, 0, l - 1, :], bank[:, 0:FM], ACT.Copy)
                    ins = act.activation(FWx[0:FX, l - 1, :], bank[0:FX, FM:2 * FM], ACT.Copy)
                else:
                    act.activation(w6[:, 0:1], bank[:, 2:3], ACT.Copy)
                    act.activation(w6[:, 2:3], bank[:, 2:3], ACT.Copy)
                    ins = act.activation(w6x[0:FX, 0:1], bank[0:FX, REM + 2:REM + 3], ACT.Copy)
                ins.then_inc(S["fw_hi"], 1)
            for k, bank in enumerate((pK, pV, pH)):
                n = min(4, T - 4 * k)
                act.wait_ge(S["ft_ps"], k + 1)
                act.activation(FT[0:20, 4 * k * P:(4 * k + n) * P], bank[0:20, 0:n * P], ACT.Copy).then_inc(S["ft_ok"], 1)
            for k in range(STEPS - FC):
                act.wait_ge(S["f_mm"], k + 1)
                act.activation(H[:, 0, k % FC, :], fmain[k % 3][:, :], ACT.Relu).then_inc(S["f_hi"], 1)
                act.activation(Rr[0:3 * REM, k % FC, :], frest[k % 3][0:3 * REM, :], ACT.Relu).then_inc(S["f_hi"], 1)

            act.wait_ge(S["f6_mm"], 1)
            act.wait_ge(S["ld_q1"], 16 + after["ld_q1"])
            act.activation(Wq[:, 0], qbuf[:, 0:4, :], ACT.Copy).then_inc(S["q1_hi"], 1)
            act.wait_ge(S["ld_u1"], 16 + after["ld_u1"])
            act.activation(Wu[:, 0], qbuf[:, 8, 0:KC * RANK].rearrange("p (c n) -> p c n", c=KC), ACT.Copy).then_inc(S["u1_hi"], 1)
            ln_sqrt(3)
            act.wait_ge(S["ln_ok"], 3)

            def norm1(t, u, first=False):
                if not first:
                    act.wait_ge(S["n_ps"], t - 1 + after["n_ps"])
                act.activation(xn[:, u, :], row(nodes, t), ACT.Identity,
                               bias=nmr[:, ds(t, 1)], scale=rstd[:, ds(t, 1)]).then_inc(S["n_xn"], 1)

            def xt1_hi(t, u, first=False):
                act.wait_ge(S["n_ps"], t + 1 + after["n_ps"])
                if not first:
                    act.wait_ge(S["nu_mm"], t - 1 + after["nu_mm"])
                act.activation(xT[:, u, 0], pT[:, :].rearrange("p (c n) -> p c n", c=KC), ACT.Copy).then_inc(S["n_hi"], 1)

            def tile1(t, u, first=False, last=False):
                act.wait_ge(S["nq_sub"], t + 1 + after["nq_sub"])
                act.activation(row(qbuf, t), qx[:, u, :], ACT.Exp).then_inc(S["nq_exp"], 1)
                if not last:
                    xt1_hi(t + 1, 1 - u, first)
                act.wait_ge(S["nk_mm"], t + 1 + after["nk_mm"])
                if not first:
                    act.wait_ge(S["nk_elu"], t + after["nk_elu"])
                act.activation(et[:], pK[:, :], ACT.Exp).then_inc(S["nk_er"], 1)
                act.activation(rt[:], pK[:, :], ACT.Relu).then_inc(S["nk_er"], 1)
                act.wait_ge(S["nu_mm"], t + 1 + after["nu_mm"])
                act.activation(uhl[:, ds(t, 1), 0:RANK].rearrange("p a n -> p (a n)"), pV[:, 0:RANK], ACT.Copy).then_inc(S["nu_hi"], 1)

            norm1(0, 0, True)
            norm1(1, 1, True)
            xt1_hi(0, 0, True)
            tile1(0, 0, True)
            norm1(2, 0)
            tile1(1, 1)
            norm1(3, 1)
            with act.Fori(1, ITER - 1) as i:
                for u in range(2):
                    tile1(2 * i + u, u)
                    norm1(2 * i + u + 2, u)
            tile1(T - 2, 0)
            tile1(T - 1, 1, last=True)

            act.wait_ge(S["cmb_ps"], 1 + after["cmb_ps"])
            act.activation(kmaxb[:], pA[:, :], ACT.Copy).then_inc(S["cmb_ok"], 1)

            def znorm(t, u, first=False):
                if not first:
                    act.wait_ge(S["z_xlo"], t - 1)
                act.activation(xn[:, u, :], row(nodes, t), ACT.Identity,
                               bias=nmr[:, ds(t, 1)], scale=rstd[:, ds(t, 1)]).then_inc(S["z_xn"], 1)

            def zhi(t, u, first=False):
                act.wait_ge(S["z_xn"], t + 1 + after["z_xn"])
                if not first:
                    act.wait_ge(S["z_mm"], t - 1 + after["z_mm"])
                act.activation(xT[:, u, 0].rearrange("p c n -> p (c n)"), xn[:, u, :], ACT.Copy).then_inc(S["z_xhi"], 1)

            def zexp(t, u, first=False):
                act.wait_ge(S["z_sub"], t + 1 + after["z_sub"])
                if not first:
                    act.wait_ge(S["z_klo"], t - 1 + after["z_klo"])
                act.activation((et, rt)[u][:], row(kbuf, t), ACT.Exp).then_inc(S["z_exp"], 1)
                act.wait_ge(S["z_exp"], t + 1 + after["z_exp"])
                act.activation(khl2[:, u, 0, :], (et, rt)[u][:], ACT.Copy).then_inc(S["z_khi"], 1)

            for t in range(2):
                znorm(t, t, True)
                zhi(t, t, True)
                zexp(t, t, True)
            with act.Fori(1, ITER) as i:
                for u in range(2):
                    znorm(2 * i + u, u)
                    zhi(2 * i + u, u)
                    zexp(2 * i + u, u)

            act.wait_ge(S["zr_ok"], 1 + after["zr_ok"])
            for b, bank in enumerate((pK, pV)):
                act.activation(xn[:, b, :], bank[:, :], ACT.Copy, scale=ksum[:, b:b + 1]).then_inc(S["zs_a"], 1)
            act.wait_ge(S["zt_ps"], 1 + after["zt_ps"])
            for c, bank in enumerate((pT, pA, pKV[0], pKV[1])):
                act.activation(ZT[:, 0, c, :], bank[:, :], ACT.Copy).then_inc(S["zt_hi"], 1)
            act.wait_ge(S["kt_mm"], 1 + after["kt_mm"])
            act.wait_ge(S["kz"], 1)
            for h in range(2):
                r = slice(h * DH, (h + 1) * DH)
                act.activation(xT[r, 0, 0, :, r], pK[r, :].rearrange("p (c n) -> p c n", c=KC)[:, :, r], ACT.Copy).then_inc(S["kt_hi"], 1)
            for p, bank in enumerate((pV, pH, pQ, pT)):
                act.wait_ge(S["mw_mm"], p + 1 + after["mw_mm"])
                act.activation(MW[:, 0, p, :], bank[:, :], ACT.Copy).then_inc(S["mw_hi"], 1)
            act.wait_ge(S["ld_v2"], 32 + after["ld_v2"])
            act.activation(Vt[:, 0, :], vraw[:], ACT.Copy).then_inc(S["vt_hi"], 1)

            def a2_hi(t, u, c):
                n, b = min(4, T - 4 * c), chunk_bank(u, c)
                act.wait_ge(S["a2_ps"], 3 * t + c + 1)
                act.activation(ATs[:, u, 0, 4 * c:4 * c + n, :], b[:, 0:n * P].rearrange("p (s n) -> p s n", n=P), ACT.Copy).then_inc(S["a2_hi"], 1)

            def r2_hi(t, u, first=False):
                act.wait_ge(S["r2_ps"], t + 1 + after["r2_ps"])
                if not first:
                    act.wait_ge(S["m2_mm"], t - 1 + after["m2_mm"])
                act.activation(xT[:, u, 0], pT[:, :].rearrange("p (c n) -> p c n", c=KC), ACT.Copy).then_inc(S["r2_hi"], 1)

            def g2_hi(t, u, first=False):
                act.wait_ge(S["a2_mm"], t + 1 + after["a2_mm"])
                if not first:
                    act.wait_ge(S["s2_mm"], t - 1 + after["s2_mm"])
                act.activation(agT[:, u, 0, :], pKV[0][:, 0:P], ACT.Copy, scale=s2[:, 0:1]).then_inc(S["g2_hi"], 1)

            act.wait_ge(S["ld_small"], 48)
            for t in range(2):
                for c in range(3):
                    a2_hi(t, t, c)
            g2_hi(0, 0, True)
            r2_hi(0, 0, True)

            def sums1(t, u, first=False, ahead=True):
                if ahead:
                    a2_hi(t + 2, u, 0)
                    a2_hi(t + 2, u, 1)
                g2_hi(t + 1, 1 - u, first)
                if ahead:
                    a2_hi(t + 2, u, 2)
                r2_hi(t + 1, 1 - u, first)

            sums1(0, 0, True)
            sums1(1, 1)
            with act.Fori(1, ITER - 1) as i:
                for u in range(2):
                    sums1(2 * i + u, u)
            sums1(T - 2, 0, ahead=False)

            ln_sqrt(4)
            for k, bank in enumerate((pKV[0], pT)):
                act.wait_ge(S["f1_ps"], k + 1)
                act.activation(f1T[:, 0, 2 * k:2 * k + 2, :], bank[:, :].rearrange("p (c n) -> p c n", c=2), ACT.Copy).then_inc(S["f1_hi"], 1)
            act.wait_ge(S["f2_ps"], 1)
            act.activation(f2T[:, 0], pKV[1][:, :].rearrange("p (c n) -> p c n", c=2), ACT.Copy, scale=0.5).then_inc(S["f2_hi"], 1)
            act.wait_ge(S["ln_ok"], 4)
            for g in range(3):
                t0, t1 = 4 * g, min(4 * g + 4, T)
                act.wait_ge(S["s_add"], g + 1)
                for t in range(t0, t1):
                    act.activation(sn[:, t, :], sn[:, t, :], ACT.Identity, bias=nmr2[:, t:t + 1], scale=rstd[:, t:t + 1]).then_inc(S["s_n"], 1)
                act.wait_ge(S["s_n"], t1)
                act.activation(shl[:, 0, t0:t1, :], sn[:, t0:t1, :], ACT.Copy).then_inc(S["s_hi"], 1)
            act.wait_ge(S["w1_mm"], 1)
            act.activation(W1[:, 0], pA[:, :].rearrange("p (c n) -> p c n", c=2), ACT.Copy).then_inc(S["w1_hi"], 1)
            for g in range(3):
                n = min(4, T - 4 * g)
                act.wait_ge(S["ll_mm"], g + 1)
                act.activation(llT[:, 0, :, 4 * g * DH:(4 * g + n) * DH].rearrange("p i (t r) -> p i t r", r=DH),
                               (pK, pV, pH)[g][:, 0:n * P].rearrange("p (t i r) -> p i t r", i=2, r=DH), ACT.Copy).then_inc(S["ll_hi"], 1)
            for g in range(3):
                n = min(4, T - 4 * g) * DH
                r = slice(4 * g * DH, 4 * g * DH + n)
                act.wait_ge(S["hh_mm"], g + 1)
                for b in range(2):
                    act.activation(hf[:, b, r], (pQ, pA, pT)[g][:, b * HALF:b * HALF + n], ACT.Gelu, bias=fb1[:, b:b + 1]).then_inc(S["hh_g"], 1)
                act.wait_ge(S["hh_g"], 2 * g + 2)
                for b in range(2):
                    act.activation(hT[:, 0, b, 8 * g * DH:8 * g * DH + 2 * n].rearrange("p (r v) -> p r v", v=2),
                                   hf[:, b, r].rearrange("p (r v) -> p r v", v=1).broadcast_to([P, n, 2]), ACT.Copy).then_inc(S["hh_hi"], 1)

        @block.gpsimd
        def _(pool):
            pool.memset(erow[:], 0).then_inc(S["pad_zero"], 1)
            pool.wait_ge(S["pad_zero"], 1)
            pool.memset(nodes[96:P, T - 1, :], 0.0).then_inc(S["pad_zero"], 1)
            pool.wait_ge(S["pad_zero"], 2)
            pool.memset(onesf[:], 1.0).then_inc(S["c_pool"], 1)
            pool.wait_ge(S["c_pool"], 1)
            pool.affine_select(out=ident[:], in_=onesf[:], compare_op=ALU.is_equal, fill=0.0, base=0,
                               pattern=[[-1, P]], channel_multiplier=1).then_inc(S["consts"], 1)
            pool.iota(iota_src[:], pattern=[[1, P]], base=0, channel_multiplier=0,
                      allow_small_or_imprecise_dtypes=True).then_inc(S["consts"], 1)
            pool.iota(iota_key[:], pattern=[[1, T * WIN]], base=0, channel_multiplier=0,
                      allow_small_or_imprecise_dtypes=True).then_inc(S["consts"], 1)
            pool.memset(vhl[:, 0, :, P:VC].bitcast(F32), 1.0).then_inc(S["consts"], 1)
            pool.memset(vhl[:, 1, :, P:VC].bitcast(F32), 0.0).then_inc(S["consts"], 1)
            pool.memset(ones2[:].bitcast(F32), 1.0).then_inc(S["consts"], 1)
            pool.memset(AT[:], 0.0).then_inc(S["at_zero"], 1)

            def weigh(g, r):
                pool.wait_ge(S["oh_src"], g + 1)
                w = whl[:, ds(2 * g, 2), :].bitcast(F32).rearrange("p c (k n) -> p c k n", n=1).broadcast_to([P, 2, 2, P])
                o = onehot_[:, r].rearrange("p c (k n) -> p c k n", k=1).broadcast_to([P, 2, 2, P])
                pool.tensor_tensor(Loh[:, r], o, w, ALU.mult).then_inc(S["oh_pool"], 1)

            for k in (1, 2):
                pool.wait_ge(S["w_hi"], k + 1)
                pool.tensor_tensor(wsl[:, k, 1], wraw[:, k, 1], wsl[:, k, 0].bitcast(F32), ALU.subtract).then_inc(S["w_lo2"], 1)
            pool.wait_ge(S["e_dve"], 1)
            with pool.Fori(0, ITER) as i:
                for j in range(CPI):
                    weigh(CPI * i + j, j % 3)

            pool.wait_ge(S["at_done"], 1)
            for s_ in range(DEG_DVE + 1, T):
                first = AT[:, DEG_DVE, :] if s_ == DEG_DVE + 1 else degp[:, 1, :]
                pool.tensor_tensor(degp[:, 1, :], first, AT[:, s_, :], ALU.add).then_inc(S["degp_pool"], 1)
                pool.wait_ge(S["degp_pool"], s_ - DEG_DVE)
            pool.wait_ge(S["wo_hi"], 1)
            pool.tensor_tensor(WO[:, 1], raw[:], WO[:, 0].bitcast(F32), ALU.subtract).then_inc(S["wo_lo"], 1)

            def ats_lo(t, u):
                pool.wait_ge(S["ats_hi"], t + 1)
                pool.tensor_tensor(ATs[:, u, 1], AT[:, :, ds(t * P, P)], ATs[:, u, 0].bitcast(F32),
                                   ALU.subtract).then_inc(S["ats_lo"], 1)

            def x_bias(i, u):
                pool.wait_ge(S[f"x_ld{u}"], 16 * (i + 1))
                pool.tensor_tensor(xb[:, u, :], xb[:, u, :], brow[:, 0, :], ALU.add).then_inc(S["xb_ok"], 1)

            ats_lo(0, 0)
            ats_lo(1, 1)
            pool.wait_ge(S["b_ld"], 32)
            pool.tensor_tensor(brow[:, 0, :], brow[:, 0, :], brow[:, 1, :], ALU.add).then_inc(S["bias_ok"], 1)
            pool.wait_ge(S["bias_ok"], 1)
            x_bias(0, 0)
            x_bias(0, 1)
            with pool.Fori(1, ITER - 1) as i:
                for u in range(2):
                    ats_lo(2 * i + u, u)
                    x_bias(i, u)
            ats_lo(T - 2, 0)
            x_bias(ITER - 1, 0)
            ats_lo(T - 1, 1)

            k = [0]

            def st(ins):
                k[0] += 1
                ins.then_inc(S["fp"], 1)
                pool.wait_ge(S["fp"], k[0])

            st(pool.iota(iota16[:], pattern=[[1, 16]], base=0, channel_multiplier=0, allow_small_or_imprecise_dtypes=True))
            pool.iota(wt16[:], pattern=[[0, 4], [-1, 16]], base=16, channel_multiplier=0,
                      allow_small_or_imprecise_dtypes=True).then_inc(S["init2"], 1)
            pool.wait_ge(S["init2"], 1)
            st(pool.memset(N0[:], 0.0))
            pool.wait_ge(S["fw_ld"], 16 * 8)
            B0 = P + 3 * REM
            for half, (nat, rows, L) in enumerate(((N1, P, FFL), (N2, 3 * REM, FFL - 1))):
                n, h = nat[0:rows, 0:L], hin[0:rows, 0:L]
                st(pool.tensor_copy(h[:, :, 0:REM], n[:, :, P:P + REM]))
                st(pool.tensor_copy(h[:, :, REM:REM + 1], n[:, :, B0:B0 + 1]))
                st(pool.tensor_copy(n[:, :, P + REM:P + 2 * REM], n[:, :, P:P + REM]))
                st(pool.tensor_tensor(n[:, :, P + 2 * REM:P + 3 * REM], n[:, :, P:P + REM], h[:, :, 0:REM].bitcast(F32), ALU.subtract))
                st(pool.tensor_tensor(n[:, :, B0 + 1:B0 + 2], n[:, :, B0:B0 + 1], h[:, :, REM:REM + 1].bitcast(F32), ALU.subtract))
                g, gh, gl = w3[0:rows, half], w3h[0:rows, half], w3l[0:rows, half]
                st(pool.tensor_copy(g[:, 0:2], n[:, 0, 0:2]))
                st(pool.tensor_copy(g[:, 2:3], n[:, 0, 30:31]))
                st(pool.tensor_copy(g[:, 3:4], n[:, 0, B0:B0 + 1]))
                st(pool.tensor_copy(gh, g))
                st(pool.tensor_tensor(gl, g, gh.bitcast(F32), ALU.subtract))
                for pos in range(2):
                    z = N0[0:rows, half, pos]
                    for blk in range(3):
                        st(pool.tensor_copy(z[:, 6 * blk + 3 * pos:6 * blk + 3 * pos + 3], (gl if blk == 2 else g)[:, 0:3]))
                    st(pool.tensor_copy(z[:, 18:19], g[:, 3:4]))
                    ins = pool.tensor_copy(z[:, 19:20], gl[:, 3:4])
                    st(ins)
                pool.engine_nop().then_inc(S["fn_ok"], 1)
            x_bias(ITER - 1, 1)
            pool.wait_ge(S["mix_mm"], T)
            pool.wait_ge(S["xb_ok"], T)
            pool.memset(Rr[96:P].bitcast(F32), 1.0).then_inc(S["pads_ok"], 1)
            pool.wait_ge(S["pads_ok"], 1)
            pool.memset(w6[:, 3:4].bitcast(F32), 0.0).then_inc(S["pads_ok"], 1)
            pool.memset(w6x[:, 1:2].bitcast(F32), 0.0).then_inc(S["pads_ok"], 1)
            for t in range(T):
                if t == 0:
                    pool.wait_ge(S["x128_ok"], 1)
                pool.tensor_scalar(nodes[:, t, :], nodes[:, t, :], small[:, 1, t:t + 1], nmr[:, t:t + 1],
                                   ALU.mult, ALU.add).then_inc(S["y_ok"], 1)

            pool.wait_ge(S["ld_v1"], 16 + after["ld_v1"])
            pool.tensor_copy(Wv[:, 0], raw[:]).then_inc(S["v1_hi"], 1)
            pool.wait_ge(S["v1_hi"], 1)
            pool.tensor_tensor(Wv[:, 1], raw[:], Wv[:, 0].bitcast(F32), ALU.subtract).then_inc(S["v1_lo"], 1)
            pool.wait_ge(S["ld_k1"], 16 + after["ld_k1"])
            pool.wait_ge(S["f_mm"], FC)
            pool.tensor_copy(Wk[:, 0], qbuf[:, 4:8, :]).then_inc(S["k1_hi"], 1)
            pool.wait_ge(S["k1_hi"], 1 + after["k1_hi"])
            pool.tensor_tensor(Wk[:, 1], qbuf[:, 4:8, :], Wk[:, 0].bitcast(F32), ALU.subtract).then_inc(S["k1_lo"], 1)
            pool.memset(rows1[:, 0, :].bitcast(F32), 1.0).then_inc(S["c1"], 1)
            pool.memset(rows1[:, 1, :].bitcast(F32), 0.5).then_inc(S["c1"], 1)
            pool.tensor_scalar(lomask[:], ident[:, 1:2], -1.0, None, ALU.mult).then_inc(S["c1"], 1)
            st(pool.memset(pairs[:], -0.25))
            pv = pairs[:].rearrange("p (r v) -> p r v", v=2)
            st(pool.affine_select(out=pv, in_=pv, compare_op=ALU.is_ge, fill=0.0, base=0, pattern=[[-2, DH], [0, 2]], channel_multiplier=1))
            st(pool.affine_select(out=pv, in_=pv, compare_op=ALU.is_ge, fill=0.0, base=1, pattern=[[2, DH], [0, 2]], channel_multiplier=-1))
            pool.tensor_copy(pairm[:], pairs[:]).then_inc(S["c1"], 1)
            pool.tensor_scalar(pairq[:], pv[:, :, 0], -2.0, None, ALU.mult).then_inc(S["c1"], 1)
            pool.wait_ge(S["q1_hi"], 1 + after["q1_hi"])
            pool.tensor_tensor(Wq[:, 1], qbuf[:, 0:4, :], Wq[:, 0].bitcast(F32), ALU.subtract).then_inc(S["q1_lo"], 1)
            pool.wait_ge(S["u1_hi"], 1 + after["u1_hi"])
            pool.tensor_tensor(Wu[:, 1], qbuf[:, 8, 0:KC * RANK].rearrange("p (c n) -> p c n", c=KC), Wu[:, 0].bitcast(F32),
                               ALU.subtract).then_inc(S["u1_lo"], 1)
            def z_xlo(t, u):
                pool.wait_ge(S["z_xhi"], t + 1 + after["z_xhi"])
                pool.tensor_tensor(xT[:, u, 1].rearrange("p c n -> p (c n)"), xn[:, u, :], xT[:, u, 0].rearrange("p c n -> p (c n)").bitcast(F32),
                                   ALU.subtract).then_inc(S["z_xlo"], 1)

            z_xlo(0, 0)
            z_xlo(1, 1)
            pool.wait_ge(S["ld_wp"], 16 + after["ld_wp"])
            for c in range(KC):
                pool.tensor_copy(Wp[:, 0, c, :], raw[:, c, :]).then_inc(S["p1_hi"], 1)
                z_xlo(2 + 2 * (c // 2) + c % 2, c % 2)
            for c in range(KC):
                pool.wait_ge(S["p1_hi"], c + 1 + after["p1_hi"])
                pool.tensor_tensor(Wp[:, 1, c, :], raw[:, c, :], Wp[:, 0, c, :].bitcast(F32), ALU.subtract).then_inc(S["p1_lo"], 1)
                z_xlo(6 + c, c % 2)

            pool.wait_ge(S["ld_f1"], 64 + after["ld_f1"])
            pool.tensor_copy(PTh[:, 0], PTr[:]).then_inc(S["pt_hi"], 1)
            pool.wait_ge(S["pt_hi"], 1 + after["pt_hi"])
            pool.tensor_tensor(PTh[:, 1], PTr[:], PTh[:, 0].bitcast(F32), ALU.subtract).then_inc(S["pt_lo"], 1)
            pool.wait_ge(S["s_add"], 3)
            for t in range(T):
                pool.tensor_scalar(nodes[:, t, :], nodes[:, t, :], small[:, 1, t:t + 1], nmr[:, t:t + 1],
                                   ALU.mult, ALU.add).then_inc(S["y2_ok"], 1)

        @block.vector
        def _(v):
            link = [0]

            def step(ins):
                link[0] += 1
                ins.then_inc(S["sd"], 1)
                v.wait_ge(S["sd"], link[0])

            def newton(x, r, y):
                step(v.tensor_tensor(y, r, r, ALU.mult))
                step(v.tensor_tensor(y, y, x, ALU.mult))
                step(v.tensor_scalar(y, y, -0.5, 1.5, ALU.mult, ALU.add))
                step(v.tensor_tensor(r, r, y, ALU.mult))

            def aggregate_stats():
                for t in range(T):
                    ins = v.bn_aggr(mv[:, t, :], stat[:, t, :])
                step(ins)

            def ln_coefficients(n):
                var = small[:, 3, :]
                v.tensor_scalar(var, mv[:, :, 1], EPS, None, ALU.add).then_inc(S["ln_var"], 1)
                v.wait_ge(S["ln_sqrt"], n)
                step(v.reciprocal(rstd[:], rstd[:]))
                newton(var, rstd[:], small[:, 2, :])
                v.scalar_tensor_tensor(nmr[:], mv[:, :, 0], -1.0, rstd[:], ALU.mult, ALU.mult).then_inc(S["ln_ok"], 1)
                v.wait_ge(S["ln_ok"], n)

            def split_lo(i):
                v.wait_ge(S["w_hi"], i + 1)
                v.tensor_tensor(wsl[:, i, 1], wraw[:, i, 1], wsl[:, i, 0].bitcast(F32), ALU.subtract).then_inc(S["w_lo"], 1)

            def xt_lo(t, u):
                v.wait_ge(S["xt_hi"], t + 1)
                v.tensor_tensor(xT[:, u, 1, :, :], pT[:, :].rearrange("p (c n) -> p c n", c=KC),
                                xT[:, u, 0, :, :].bitcast(F32), ALU.subtract).then_inc(S["xt_lo"], 1)

            v.wait_ge(S["ld_x"], 16)
            for t in range(T):
                if t == 5:
                    v.wait_ge(S["ld_xb"], 16)
                if t == T - 1:
                    v.wait_ge(S["ld_x2"], 16)
                    v.wait_ge(S["pad_zero"], 2)
                ins = v.bn_stats(stat[:, t, :], nodes[:, t, :])
            step(ins)
            aggregate_stats()
            ln_coefficients(1)
            v.wait_ge(S["ld_edge"], 16 * 9)
            step(v.tensor_copy(frow[:, 2], erow[:, 1]))
            step(v.tensor_copy(frow[:, 3], erow[:, 2].bitcast(F32)))
            step(v.tensor_scalar(erow[:, 1], erow[:, 0], 7, None, ALU.logical_shift_right))
            step(v.tensor_scalar(erow[:, 2], erow[:, 0], P - 1, None, ALU.bitwise_and))
            step(v.tensor_scalar(frow[:, 1], erow[:, 1], float(WIN), None, ALU.mult))
            v.tensor_copy(frow[:, 0], erow[:, 2]).then_inc(S["c_dve"], 1)
            split_lo(0)
            xt_lo(0, 0)
            v.wait_ge(S["e_pe"], 1)
            dl, hi20, wf, vd = (edge[:, k, :] for k in range(4))
            c3 = lambda k: pK[:, k * CH:(k + 1) * CH]
            step(v.tensor_copy(srclo[:], c3(0)))
            step(v.tensor_copy(hi20, c3(1)))
            step(v.tensor_copy(dl, c3(2)))
            step(v.tensor_copy(rest[:, 0, :], c3(2)))
            step(v.tensor_copy(rest[:, 1, :], c3(1)))
            step(v.tensor_copy(wf, pV[:, 0:CH]))
            base = dl[0:1, :].rearrange("p (j c) -> p j c", c=2)[:, :, 0]
            step(v.tensor_copy(baseint[:], base))
            v.tensor_copy(baserow[:], base).then_inc(S["c_dve"], 1)
            v.wait_ge(S["e_pe"], 2)
            v.wait_ge(S["c_dve"], 2)
            v2 = lambda x: x.rearrange("p (j c) -> p j c", c=2)
            step(v.tensor_tensor(v2(dl), v2(dl), pH[:, 0:CP].rearrange("p (j c) -> p j c", c=1).broadcast_to([P, CP, 2]), ALU.subtract))
            step(v.tensor_scalar(vd, dl, 0.0, None, ALU.is_ge))
            step(v.scalar_tensor_tensor(vd, dl, float(WIN), vd, ALU.is_lt, ALU.mult))
            step(v.scalar_tensor_tensor(dl, dl, 1.0, hi20, ALU.add, ALU.add))
            step(v.tensor_tensor(dl, dl, vd, ALU.mult))
            step(v.tensor_scalar(key[:], dl, -1.0, None, ALU.add))
            step(v.tensor_copy(whl[:, :, 0], wf))
            v.tensor_tensor(whl[:, :, 1], wf, whl[:, :, 0].bitcast(F32), ALU.subtract).then_inc(S["e_dve"], 1)

            def onehots(g, j, first):
                slot_free(v, g, j, first)
                col, r = 2 * g, j % 3
                for c in range(2):
                    ins = v.tensor_scalar(onehot_[:, r, c, :], iota_src[:], srclo[:, ds(col + c, 1)], None, ALU.is_equal)
                ins.then_inc(S["oh_src"], 1)
                v.tensor_scalar(Roh[:, r, 1, :], iota_key[:], key[:, ds(col + 1, 1)], None,
                                ALU.is_equal).then_inc(S["oh_dve"], 1)

            def count_outside():
                step(v.tensor_scalar(vd, vd, -1.0, 1.0, ALU.mult, ALU.add))
                step(v.tensor_tensor(rest[:, 2, :], wf, vd, ALU.mult))
                step(v.tensor_scalar(vd, rest[:, 2, :], 0.0, None, ALU.not_equal))
                v.tensor_reduce(outside[:], vd, AX, ALU.add).then_inc(S["rest_ok"], 1)
                v.wait_ge(S["rest_ps"], 1)
                v.tensor_copy(flagint[:], pA[0:1, 0:1]).then_inc(S["flag_ok"], 1)

            regs = [v.alloc_register(f"window{k}") for k in range(CPI)]

            def two(i, first=False, last=False):
                v.load(regs, baseint[0:1, ds(CPI * i, CPI)])
                vals = [v.snap(r, min_val=0, max_val=N - 1) for r in regs]

                def pair(j):
                    g = CPI * i + j
                    if not (last and j >= CPI - 2):
                        onehots(g + 2, (j + 2) % CPI, first and j < CPI - 2)
                    v.wait_ge(S["a_mm"], g + 1)
                    if later(g, 1):
                        v.wait_ge(S["a_acc"], g)
                    win = AT[:, :, ds(vals[j], WIN)]
                    v.tensor_tensor(win, win, pA[:, 0:T * WIN].rearrange("p (s w) -> p s w", s=T), ALU.add)\
                     .then_inc(S["a_acc"], 1)

                at = 0
                for u in range(2):
                    t = 2 * i + u
                    for k in range(4):
                        upto = pairs_by(4 * u + k + 1, first)
                        if k < 3 and not (first and u == 0):
                            upto += 1
                        if first and u == 1 and k == 0:
                            v.wait_ge(S["at_zero"], 1)
                        while at < upto:
                            pair(at)
                            at += 1
                        qv = qbuf[:, ds(t, 1), :].rearrange("p a n -> p (a n)")
                        if k == 0:
                            v.wait_ge(S["q_er"], 2 * t + 2)
                            v.scalar_tensor_tensor(qv, et[:], 1.0, qv, ALU.min, ALU.add).then_inc(S["q_elu"], 1)
                        elif k == 1:
                            v.wait_ge(S["k_er"], 2 * t + 2)
                            v.scalar_tensor_tensor(rt[:], et[:], 1.0, rt[:], ALU.min, ALU.add).then_inc(S["k_elu"], 1)
                        elif k == 2:
                            v.wait_ge(S["v_hi"], t + 1)
                            v.tensor_tensor(vhl[:, 1, :, 0:P], pV[:, :].rearrange("p (c n) -> p c n", c=PAIRS),
                                            vhl[:, 0, :, 0:P].bitcast(F32), ALU.subtract).then_inc(S["v_lo"], 1)
                            v.wait_ge(S["k_hi"], t + 1)
                            v.tensor_tensor(khl[:, 1, :], rt[:], khl[:, 0, :].bitcast(F32), ALU.subtract).then_inc(S["k_lo"], 1)
                            if not (last and u == 1):
                                xt_lo(t + 1, 1 - u)
                            if first and u == 0:
                                count_outside()
                                onehots(0, 0, True)
                                onehots(1, 1, True)
                while at < CPI:
                    pair(at)
                    at += 1

            split_lo(3)
            two(0, first=True)
            with v.Fori(1, ITER - 1) as i:
                two(i)
            two(ITER - 1, last=True)

            count_reg = v.alloc_register("outside")
            v.wait_ge(S["flag_ok"], 1)
            v.load(count_reg, flagint[0:1, 0:1])
            with v.If(v.snap(count_reg, min_val=0, max_val=CH * P) > 0):
                v.wait_ge(S["a_acc"], CP)
                v.tensor_copy(whl[:, :, 0], rest[:, 2, :]).then_inc(S["rs"], 1)
                v.wait_ge(S["rs"], 1)
                v.tensor_tensor(whl[:, :, 1], rest[:, 2, :], whl[:, :, 0].bitcast(F32), ALU.subtract).then_inc(S["rs"], 1)
                v.wait_ge(S["rs"], 2)
                with v.Fori(0, NP // WIN) as w:
                    def st(n, ins):
                        ins.then_inc(S["rs"], 1)
                        if n < 6:
                            v.wait_ge(S["rs"], 6 * w + (2 + n))
                    d = rest[:, 0, :]
                    st(1, v.tensor_scalar(key[:], d, 0.0, None, ALU.is_ge))
                    st(2, v.scalar_tensor_tensor(key[:], d, float(WIN), key[:], ALU.is_lt, ALU.mult))
                    st(3, v.scalar_tensor_tensor(rest[:, 2, :], d, 1.0, rest[:, 1, :], ALU.add, ALU.add))
                    st(4, v.tensor_tensor(key[:], key[:], rest[:, 2, :], ALU.mult))
                    st(5, v.tensor_scalar(key[:], key[:], -1.0, None, ALU.add))
                    st(6, v.tensor_scalar(d, d, -float(WIN), None, ALU.add))
                    with v.Fori(0, CP) as g:
                        v.wait_ge(S["rs"], 6 * w + 8)
                        for c in range(2):
                            col = 2 * g + c
                            for part in range(2):
                                v.tensor_scalar(Loh[:, 0, c, part, :], iota_src[:], srclo[:, ds(col, 1)],
                                                whl[:, ds(col, 1), part].bitcast(F32), ALU.is_equal, ALU.mult)
                            ins = v.tensor_scalar(Roh[:, 0, c, :], iota_key[:], key[:, ds(col, 1)], None, ALU.is_equal)
                        ins.then_inc(S["rest_oh"], 1)
                        v.wait_ge(S["rest_mm"], CP * w + g + 1)
                        win = AT[:, :, ds(WIN * w, WIN)]
                        v.tensor_tensor(win, win, pA[:, 0:T * WIN].rearrange("p (s w) -> p s w", s=T), ALU.add)\
                         .then_inc(S["rest_acc"], 1)
                        v.wait_ge(S["rest_acc"], CP * w + g + 1)

            def kv_blocks():
                step(v.memset(rt[:], 0.0))
                for b in range(2):
                    for h in range(2):
                        r = slice(h * DH, (h + 1) * DH)
                        o = rt[r, 2 * b * P:(2 * b + 2) * P].rearrange("p (c n) -> p c n", c=2)[:, :, r]
                        i_ = pKV[b][r, 0:2 * VC].rearrange("p (c n) -> p c n", c=2)
                        step(v.tensor_copy(o, i_[:, :, r]))
                    step(v.tensor_copy(ksum[:, 2 * b:2 * b + 2], pKV[b][:, 0:2 * VC].rearrange("p (c n) -> p c n", c=2)[:, :, P]))

            v.wait_ge(S["a_acc"], CP)
            v.engine_nop().then_inc(S["at_done"], 1)
            v.tensor_reduce(degp[:, 0, :], AT[:, 0:DEG_DVE, :].rearrange("p s d -> p d s"), AX, ALU.add).then_inc(S["degp_ok"], 1)
            v.wait_ge(S["degp_ok"], 1)
            v.wait_ge(S["degp_pool"], T - DEG_DVE - 1)
            v.tensor_tensor(degp[:, 0, :], degp[:, 0, :], degp[:, 1, :], ALU.add).then_inc(S["degp_ok"], 1)
            v.wait_ge(S["kv_mm"], T)
            kv_blocks()
            for p in range(PAIRS):
                ins = v.tensor_scalar(et[:, p * P:(p + 1) * P], onesf[:], ksum[:, p:p + 1], None, ALU.mult)
            ins.then_inc(S["bd_ok"], 1)
            v.wait_ge(S["dhl_hi"], 1)
            v.tensor_tensor(dhl[:, 1, :], degp[:, 0, :], dhl[:, 0, :].bitcast(F32), ALU.subtract).then_inc(S["dhl_lo"], 1)
            v.wait_ge(S["kvt_hi"], 1)
            v.tensor_tensor(xT[:, 0, 1], pT[:, :].rearrange("p (c n) -> p c n", c=KC), xT[:, 0, 0].bitcast(F32),
                            ALU.subtract).then_inc(S["kvt_lo"], 1)
            qs = [xn[:, 1, :], rt[:]]

            def heads(x):
                return x.rearrange("p (h d) -> p h d", h=HEADS)

            def q_scaled(t, u, at, first=False):
                k = [0]

                def st(ins):
                    k[0] += 1
                    ins.then_inc(S["sd"], 1)
                    v.wait_ge(S["sd"], at + k[0])
                qv = qbuf[:, ds(t, 1), :].rearrange("p a n -> p (a n)")
                st(v.tensor_tensor(et[:], qv, xn[:, 0, :], ALU.mult))
                st(v.tensor_reduce(den[:], heads(et[:]), AX, ALU.add))
                st(v.tensor_scalar(den[:], den[:], 1e-6, None, ALU.add))
                st(v.reciprocal(den[:], den[:]))
                if not first:
                    v.wait_ge(S["qt_ps"], t - 1)
                v.tensor_tensor(heads(qs[u]), heads(qv), den[:].rearrange("p (h d) -> p h d", d=1).broadcast_to([P, HEADS, DH]),
                                ALU.mult).then_inc(S["qs_ok"], 1)

            v.wait_ge(S["ksb_ok"], 1)
            q_scaled(0, 0, link[0], True)
            link[0] += 4
            v.wait_ge(S["deg_ps"], 1)
            d, r, m, y = deg[:], dinv[:], small[:, 1, :], small[:, 2, :]
            step(v.tensor_scalar(d, pA[:, 0:2 * T].rearrange("p (t n) -> p t n", n=2)[:, :, 0], 1.0, None, ALU.add))
            v.tensor_scalar(small[:, 0, :], d, 1e-30, None, ALU.max).then_inc(S["deg_ok"], 1)
            v.wait_ge(S["deg_sqrt"], 1)

            step(v.reciprocal(r, r))
            newton(small[:, 0, :], r, y)
            step(v.tensor_scalar(m, d, 0.0, None, ALU.is_gt))
            step(v.tensor_tensor(r, r, m, ALU.mult))
            v.tensor_tensor(dinv2[:], r, r, ALU.mult).then_inc(S["dinv_ok"], 1)
            for t in range(T):
                v.wait_ge(S["g_hi"], t + 1)
                v.scalar_tensor_tensor(G[:, 1, t, :], nodes[:, t, :], dinv[:, t:t + 1], G[:, 0, t, :].bitcast(F32),
                                       ALU.mult, ALU.subtract).then_inc(S["g_lo"], 1)

            for p, bank in enumerate(mbank):
                v.wait_ge(S["m_hi"], p + 1)
                v.tensor_tensor(WO[:, 1, p, :], bank[:, :], WO[:, 0, p, :].bitcast(F32), ALU.subtract).then_inc(S["m_lo"], 1)

            def qt_lo(t, u):
                v.wait_ge(S["qt_hi"], t + 1)
                v.tensor_tensor(xT[:, u, 1], pT[:, :].rearrange("p (c n) -> p c n", c=KC), xT[:, u, 0].bitcast(F32),
                                ALU.subtract).then_inc(S["qt_lo"], 1)

            def total(t, u, at):
                k = [0]

                def st(ins):
                    k[0] += 1
                    ins.then_inc(S["sd"], 1)
                    v.wait_ge(S["sd"], at + 4 + k[0])
                nv = nodes[:, ds(t, 1), :].rearrange("p a n -> p (a n)")
                v.wait_ge(S["xb_ok"], t + 1)
                st(v.scalar_tensor_tensor(nv, nv, dinv2[:, ds(t, 1)], xb[:, u, :], ALU.mult, ALU.add))
                v.wait_ge(S["agg_mm"], t + 1)
                st(v.scalar_tensor_tensor(nv, pG[u][:, :], dinv[:, ds(t, 1)], nv, ALU.mult, ALU.add))
                v.wait_ge(S["mix_mm"], t + 1)
                v.tensor_tensor(nv, nv, pM[u][:, :], ALU.add).then_inc(S["x1_ok"], 1)
                v.wait_ge(S["x1_ok"], t + 1)
                v.bn_stats(stat[:, ds(t, 1), :].rearrange("p a n -> p (a n)"), row(nodes, t)).then_inc(S["sd"], 1)

            PER = 7
            base = link[0]
            q_scaled(1, 1, base, True)
            qt_lo(0, 0)
            qt_lo(1, 1)
            total(0, 0, base)
            with v.Fori(1, ITER - 1) as i:
                for u in range(2):
                    g = 2 * i + u
                    q_scaled(g, u, base + PER * (g - 1))
                    qt_lo(g, u)
                    total(g - 1, 1 - u, base + PER * (g - 1))
            for g in (T - 2, T - 1):
                q_scaled(g, g % 2, base + PER * (g - 1))
                qt_lo(g, g % 2)
                total(g - 1, 1 - g % 2, base + PER * (g - 1))
            total(T - 1, 1, base + PER * (T - 1) - 4)

            link[0] = base - 4 + PER * T

            v.wait_ge(S["sd"], link[0])
            aggregate_stats()
            ln_coefficients(2)
            step(v.tensor_scalar(small[:, 1, :], rstd[:], 1.0, None, ALU.add))
            for t in range(T):
                ins = v.tensor_scalar(X128[:, t, :], nodes[:, t, 0:P], rstd[:, t:t + 1], nmr[:, t:t + 1], ALU.mult, ALU.add)
            ins.then_inc(S["x128_ok"], 1)
            v.wait_ge(S["x128_ok"], 1)
            v.wait_ge(S["init2"], 1)
            x16 = X128[:, :, 64:P]
            w16 = wt16[:].rearrange("p g j -> p (g j)").rearrange("p (a n) -> p a n", a=1).broadcast_to([P, T, 64])
            step(v.tensor_copy(F6[:, :, 2:3], X128[:, :, 29:30]))
            step(v.tensor_copy(F6[:, :, 5:6], X128[:, :, 29:30]))
            step(v.tensor_scalar(mask2[:], X128[:, :, 0], 0.5, 2.0, ALU.is_ge, ALU.mult))
            step(v.scalar_tensor_tensor(mask2[:], X128[:, :, 1], 0.5, mask2[:], ALU.is_ge, ALU.mult))
            step(v.scalar_tensor_tensor(x16, x16, 0.5, w16, ALU.is_gt, ALU.mult))
            step(v.tensor_reduce(first1[:], x16.rearrange("p t (g j) -> p t g j", g=4), AX, ALU.max))
            step(v.tensor_scalar(first1[:], first1[:], -1.0, 16.0, ALU.mult, ALU.add))
            step(v.scalar_tensor_tensor(first1[:], first1[:], 16.0, first1[:], ALU.is_lt, ALU.mult))
            step(v.tensor_copy(F6[:, :, 0:4:3], first1[:, :, 0:2]))
            step(v.tensor_copy(F6[:, :, 1:5:3], first1[:, :, 2:4]))
            step(v.tensor_copy(hif[:], F6[:]))
            step(v.tensor_copy(F20[:, :, 0:6], hif[:].bitcast(F32)))
            step(v.tensor_copy(F20[:, :, 12:18], hif[:].bitcast(F32)))
            step(v.tensor_tensor(F20[:, :, 6:12], F6[:], hif[:].bitcast(F32), ALU.subtract))
            v.memset(F20[:, :, 18:20], 1.0).then_inc(S["f20_ok"], 1)
            for l in range(1, FFL):
                bank = wbank[l]
                v.wait_ge(S["fw_hi"], l + 1)
                if l < FFL - 1:
                    v.tensor_tensor(FWm[:, 1, l - 1, :], bank[:, 0:FM], FWm[:, 0, l - 1, :].bitcast(F32), ALU.subtract).then_inc(S["fw_lo"], 1)
                else:
                    v.tensor_tensor(w6[:, 1:2], bank[:, 2:3], w6[:, 0:1].bitcast(F32), ALU.subtract).then_inc(S["fw_lo"], 1)

            def part_stats(t):
                v.wait_ge(S["y_ok"], t + 1)
                v.bn_stats(st3[:, t, 0, :], nodes[:, t, 0:P])
                v.bn_stats(st3[:, t, 1, :], nodes[:, t, P + 32:D])

            for k in range(STEPS - FC):
                v.wait_ge(S["f_hi"], 2 * k + 2)
                v.scalar_tensor_tensor(H[:, 1, k % FC, :], fmain[k % 3][:, :], 0.0, H[:, 0, k % FC, :].bitcast(F32),
                                       ALU.max, ALU.subtract)
                r = Rr[REM:2 * REM, k % FC, :]
                v.scalar_tensor_tensor(r, frest[k % 3][REM:2 * REM, :], 0.0, r.bitcast(F32),
                                       ALU.max, ALU.subtract).then_inc(S["f_lo"], 1)
                if 3 <= k and k % 2 and (k - 3) // 2 < T:
                    part_stats((k - 3) // 2)
            v.wait_ge(S["f6_mm"], 1)
            r6 = pKV[0][:, 0:4 * FC * 2].rearrange("p (c q u n) -> p c q u n", c=FC, q=2, u=2)
            for pos in range(2):
                ro = res[:, :, pos].rearrange("p (c u) -> p c u", u=2)
                step(v.tensor_copy(ro, r6[:, :, pos, :, 0]))
                step(v.tensor_tensor(ro, ro, r6[:, :, pos, :, 1], ALU.add))
            step(v.tensor_scalar(res[:], res[:], 0.0, 15.0, ALU.max, ALU.min))
            step(v.tensor_scalar(res[:], res[:], ROUND, ROUND, ALU.add, ALU.subtract))
            o16 = oneh[:].rearrange("p t (q j) -> p (t q) j", q=2)
            io = iota16[:].rearrange("p (a j) -> p a j", a=1).broadcast_to([P, 2 * T, 16])
            rb = res[:].rearrange("p t q -> p (t q)").rearrange("p (a n) -> p a n", n=1).broadcast_to([P, 2 * T, 16])
            step(v.tensor_tensor(o16, io, rb, ALU.is_equal))
            step(v.tensor_tensor(oneh[:], oneh[:], mask2[:].rearrange("p (t n) -> p t n", n=1).broadcast_to([P, T, 32]), ALU.mult))
            step(v.tensor_tensor(nodes[:, :, P:P + 32], nodes[:, :, P:P + 32], oneh[:], ALU.add))
            for t in range(T):
                ins = v.bn_stats(st3[:, t, 2, :], nodes[:, t, P:P + 32])
            step(ins)
            for t in range(T):
                ins = v.bn_aggr(mv[:, t, :], st3[:, t, :, :].rearrange("p a n -> p (a n)"))
            ins.then_inc(S["x2_ok"], 1)

            v.wait_ge(S["x2_ok"], 1)
            ln_coefficients(3)

            def by_head(x):
                return x.rearrange("p (h n) -> p h n", n=1).broadcast_to([P, HEADS, DH])

            def xt1_lo(t, u):
                v.wait_ge(S["n_hi"], t + 1 + after["n_hi"])
                v.tensor_tensor(xT[:, u, 1], pT[:, :].rearrange("p (c n) -> p c n", c=KC), xT[:, u, 0].bitcast(F32),
                                ALU.subtract).then_inc(S["n_lo"], 1)

            v.memset(kmax[:], 0.0).then_inc(S["kmax_z"], 1)
            v.wait_ge(S["kmax_z"], 1)

            def tile1(t, u, first=False, last=False):
                v.wait_ge(S["nq_mm"], t + 1 + after["nq_mm"])
                v.tensor_reduce(den[:], heads(pQ[:, :]), AX, ALU.max).then_inc(S["sq"], 1)
                v.wait_ge(S["sq"], 2 * t + 1)
                v.tensor_tensor(heads(qx[:, u, :]), heads(pQ[:, :]), by_head(den[:]), ALU.subtract).then_inc(S["nq_sub"], 1)
                if not last:
                    xt1_lo(t + 1, 1 - u)
                v.wait_ge(S["nk_er"], 2 * t + 2 + after["nk_er"])
                v.scalar_tensor_tensor(row(kbuf, t), et[:], 1.0, rt[:], ALU.min, ALU.add).then_inc(S["nk_elu"], 1)
                v.wait_ge(S["nk_elu"], t + 1 + after["nk_elu"])
                if not first:
                    v.wait_ge(S["kmax_ok"], t)
                rows = LAST if last else P
                v.tensor_tensor(kmax[0:rows, :], kmax[0:rows, :], kbuf[0:rows, ds(t, 1), :].rearrange("p a n -> p (a n)"), ALU.max)\
                 .then_inc(S["kmax_ok"], 1)
                v.wait_ge(S["nq_exp"], t + 1 + after["nq_exp"])
                v.tensor_reduce(row(sumq, t), heads(row(qbuf, t)), AX, ALU.add).then_inc(S["sq"], 1)
                v.wait_ge(S["nu_hi"], t + 1 + after["nu_hi"])
                v.tensor_tensor(uhl[:, ds(t, 1), RANK:].rearrange("p a n -> p (a n)"), pV[:, 0:RANK],
                                uhl[:, ds(t, 1), 0:RANK].rearrange("p a n -> p (a n)").bitcast(F32), ALU.subtract).then_inc(S["nu_lo"], 1)

            xt1_lo(0, 0)
            tile1(0, 0, True)
            tile1(1, 1)
            with v.Fori(1, ITER - 1) as i:
                for u in range(2):
                    tile1(2 * i + u, u)
            tile1(T - 2, 0)
            tile1(T - 1, 1, last=True)

            v.wait_ge(S["sq"], 2 * T)
            step(v.reciprocal(sumq[:], sumq[:]))

            v.wait_ge(S["cm_ps"], 1 + after["cm_ps"])
            step(v.tensor_reduce(ksum[:], pT[:, :].rearrange("p (c n) -> p c n", c=KC), AX, ALU.max))
            for p in range(PAIRS):
                ins = v.tensor_scalar(et[:, p * P:(p + 1) * P], onesf[:], ksum[:, p:p + 1], None, ALU.mult)
            ins.then_inc(S["cm_ok"], 1)
            v.wait_ge(S["cmb_ok"], 1 + after["cmb_ok"])

            def z_sub(t):
                v.tensor_tensor(row(kbuf, t), row(kbuf, t), kmaxb[:], ALU.subtract).then_inc(S["z_sub"], 1)

            def z_lo(t, u):
                v.wait_ge(S["z_khi"], t + 1 + after["z_khi"])
                v.tensor_tensor(khl2[:, u, 1, :], (et, rt)[u][:], khl2[:, u, 0, :].bitcast(F32), ALU.subtract).then_inc(S["z_klo"], 1)

            z_sub(0)
            z_sub(1)
            with v.Fori(0, ITER - 1) as i:
                for u in range(2):
                    z_sub(2 * i + u + 2)
                    z_lo(2 * i + u, u)
            z_lo(T - 2, 0)
            z_lo(T - 1, 1)

            v.wait_ge(S["z_mm"], T + after["z_mm"])
            step(v.tensor_copy(ksum[:], pKV[0][:, 0:2 * PAIRS].rearrange("p (c n) -> p c n", n=2)[:, :, 0]))
            v.reciprocal(ksum[:], ksum[:]).then_inc(S["zr_ok"], 1)
            v.wait_ge(S["zr_ok"], 1 + after["zr_ok"])
            for b, (bank, o) in enumerate(((pH, et), (pQ, rt))):
                v.tensor_scalar(o[:], bank[:, :], ksum[:, 2 + b:3 + b], None, ALU.mult).then_inc(S["zs_d"], 1)
            v.memset(xT[:, 0].bitcast(F32), 0.0).then_inc(S["kz"], 1)
            for c, bank in enumerate((pT, pA, pKV[0], pKV[1])):
                v.wait_ge(S["zt_hi"], c + 1 + after["zt_hi"])
                v.tensor_tensor(ZT[:, 1, c, :], bank[:, :], ZT[:, 0, c, :].bitcast(F32), ALU.subtract).then_inc(S["zt_lo"], 1)
            v.wait_ge(S["kt_hi"], 2 + after["kt_hi"])
            for h in range(2):
                r = slice(h * DH, (h + 1) * DH)
                v.tensor_tensor(xT[r, 0, 1, :, r], pK[r, :].rearrange("p (c n) -> p c n", c=KC)[:, :, r],
                                xT[r, 0, 0, :, r].bitcast(F32), ALU.subtract).then_inc(S["kt_lo"], 1)
            for p, bank in enumerate((pV, pH, pQ, pT)):
                v.wait_ge(S["mw_hi"], p + 1 + after["mw_hi"])
                v.tensor_tensor(MW[:, 1, p, :], bank[:, :], MW[:, 0, p, :].bitcast(F32), ALU.subtract).then_inc(S["mw_lo"], 1)
            v.wait_ge(S["vt_hi"], 1 + after["vt_hi"])
            v.tensor_tensor(Vt[:, 1, :], vraw[:], Vt[:, 0, :].bitcast(F32), ALU.subtract).then_inc(S["vt_lo"], 1)
            v.wait_ge(S["ld_b2"], 32 + after["ld_b2"])
            v.wait_ge(S["c1"], 5)
            step(v.tensor_copy(b2[0:2, :, :], xn[0:2, :, :]))
            v.scalar_tensor_tensor(b2[0:2, :, :], b2[0:2, :, :].bitcast(F32), lomask[0:2, 0:1], xn[0:2, :, :], ALU.mult, ALU.add).then_inc(S["b2_ok"], 1)

            def softmax(t, u, first=False):
                if not first:
                    v.wait_ge(S["r2_ps"], t - 1 + after["r2_ps"])
                v.tensor_tensor(heads((et, rt)[u][:]), heads(row(qbuf, t)), by_head(row(sumq, t)), ALU.mult).then_inc(S["r2_qs"], 1)

            softmax(0, 0, True)
            softmax(1, 1, True)

            def r2_lo(t, u):
                v.wait_ge(S["r2_hi"], t + 1 + after["r2_hi"])
                v.tensor_tensor(xT[:, u, 1], pT[:, :].rearrange("p (c n) -> p c n", c=KC), xT[:, u, 0].bitcast(F32),
                                ALU.subtract).then_inc(S["r2_lo"], 1)

            def g2_lo(t, u):
                v.wait_ge(S["g2_hi"], t + 1 + after["g2_hi"])
                v.scalar_tensor_tensor(agT[:, u, 1, :], pKV[0][:, 0:P], s2[:, 0:1], agT[:, u, 0, :].bitcast(F32),
                                       ALU.mult, ALU.subtract).then_inc(S["g2_lo"], 1)

            def a2_lo(t, u, c):
                n, b = min(4, T - 4 * c), chunk_bank(u, c)
                v.wait_ge(S["a2_hi"], 3 * t + c + 1 + after["a2_hi"])
                o = ATs[:, u, :, 4 * c:4 * c + n, :]
                v.tensor_tensor(o[:, 1], b[:, 0:n * P].rearrange("p (s n) -> p s n", n=P), o[:, 0].bitcast(F32),
                                ALU.subtract).then_inc(S["a2_lo"], 1)

            def total1(t, u):
                nv = row(nodes, t)
                v.wait_ge(S["s2_mm"], t + 1 + after["s2_mm"])
                v.scalar_tensor_tensor(nv, pG[u][:, :], 0.0, nv, ALU.max, ALU.add).then_inc(S["sx"], 1)
                v.wait_ge(S["sx"], 2 * t + 1)
                v.wait_ge(S["m2_mm"], t + 1 + after["m2_mm"])
                v.tensor_tensor(nv, nv, pM[u][:, :], ALU.add).then_inc(S["x3_ok"], 1)
                v.wait_ge(S["x3_ok"], t + 1 + after["x3_ok"])
                v.bn_stats(row(stat, t), row(nodes, t)).then_inc(S["sx"], 1)

            for t in range(2):
                for c in range(3):
                    a2_lo(t, t, c)
            g2_lo(0, 0)
            r2_lo(0, 0)

            def sums1(t, u, ahead=True):
                if ahead:
                    a2_lo(t + 2, u, 0)
                    a2_lo(t + 2, u, 1)
                g2_lo(t + 1, 1 - u)
                if ahead:
                    a2_lo(t + 2, u, 2)
                r2_lo(t + 1, 1 - u)
                if ahead:
                    softmax(t + 2, u)
                total1(t, u)

            with v.Fori(0, ITER - 1) as i:
                for u in range(2):
                    sums1(2 * i + u, u)
            sums1(T - 2, 0, ahead=False)
            total1(T - 1, 1)

            v.wait_ge(S["sx"], 2 * T)
            aggregate_stats()
            ln_coefficients(4)
            step(v.tensor_scalar(small[:, 1, :], rstd[:], 1.0, None, ALU.add))
            step(v.tensor_scalar(nmr2[:], nmr[:], 2.0, None, ALU.mult))
            for g in range(3):
                t0, t1 = 4 * g, min(4 * g + 4, T)
                x2v = nodes[:, t0:t1, :].rearrange("p t (i v) -> p t i v", v=2)
                v.tensor_tensor(sn[:, t0:t1, :], x2v[:, :, :, 0], x2v[:, :, :, 1], ALU.add).then_inc(S["s_add"], 1)
            v.wait_ge(S["ld_f1"], 64 + after["ld_f1"])
            step(v.tensor_copy(b3[0:2, :], b3r[0:2, :]))
            v.scalar_tensor_tensor(b3[0:2, :], b3[0:2, :].bitcast(F32), lomask[0:2, 0:1], b3r[0:2, :], ALU.mult, ALU.add).then_inc(S["b3_ok"], 1)
            for k, bank in enumerate((pKV[0], pT)):
                v.wait_ge(S["f1_hi"], k + 1)
                v.tensor_tensor(f1T[:, 1, 2 * k:2 * k + 2, :], bank[:, :].rearrange("p (c n) -> p c n", c=2),
                                f1T[:, 0, 2 * k:2 * k + 2, :].bitcast(F32), ALU.subtract).then_inc(S["f1_lo"], 1)
            v.wait_ge(S["f2_hi"], 1)
            v.scalar_tensor_tensor(f2T[:, 1], pKV[1][:, :].rearrange("p (c n) -> p c n", c=2), 0.5, f2T[:, 0].bitcast(F32),
                                   ALU.mult, ALU.subtract).then_inc(S["f2_lo"], 1)
            for g in range(3):
                t0, t1 = 4 * g, min(4 * g + 4, T)
                v.wait_ge(S["s_hi"], g + 1)
                v.tensor_tensor(shl[:, 1, t0:t1, :], sn[:, t0:t1, :], shl[:, 0, t0:t1, :].bitcast(F32), ALU.subtract).then_inc(S["s_lo"], 1)
            v.wait_ge(S["w1_hi"], 1)
            v.tensor_tensor(W1[:, 1], pA[:, :].rearrange("p (c n) -> p c n", c=2), W1[:, 0].bitcast(F32), ALU.subtract).then_inc(S["w1_lo"], 1)
            for g in range(3):
                n = min(4, T - 4 * g)
                v.wait_ge(S["ll_hi"], g + 1)
                o = slice(4 * g * DH, (4 * g + n) * DH)
                v.tensor_tensor(llT[:, 1, :, o].rearrange("p i (t r) -> p i t r", r=DH),
                                (pK, pV, pH)[g][:, 0:n * P].rearrange("p (t i r) -> p i t r", i=2, r=DH),
                                llT[:, 0, :, o].rearrange("p i (t r) -> p i t r", r=DH).bitcast(F32), ALU.subtract).then_inc(S["ll_lo"], 1)

            def result(t):
                v.wait_ge(S["o_mm"], t + 1)
                v.wait_ge(S["y2_ok"], t + 1 + after["y2_ok"])
                nv = nodes[:, t, :].rearrange("p (i v) -> p i v", v=2)
                v.tensor_tensor(nv, nv, obank[t % 4][:, 0:HALF].rearrange("p (i v) -> p i v", v=1).broadcast_to([P, HALF, 2]), ALU.add)\
                 .then_inc(S["o_ok"], 1)

            for g in range(3):
                n = min(4, T - 4 * g) * DH
                r = slice(4 * g * DH, 4 * g * DH + n)
                for b in range(2):
                    v.wait_ge(S["hh_hi"], 2 * g + b + 1)
                    o = slice(8 * g * DH, 8 * g * DH + 2 * n)
                    v.tensor_tensor(hT[:, 1, b, o].rearrange("p (r v) -> p r v", v=2),
                                    hf[:, b, r].rearrange("p (r v) -> p r v", v=1).broadcast_to([P, n, 2]),
                                    hT[:, 0, b, o].rearrange("p (r v) -> p r v", v=2).bitcast(F32), ALU.subtract).then_inc(S["hh_lo"], 1)
            for t in range(T):
                result(t)

        @block.tensor
        def _(pe):
            pe.wait_ge(S["consts"], 6)

            def transposes(t, u):
                pe.wait_ge(S["xn_ok"], t + 1)
                if later(t, 1):
                    pe.wait_ge(S["xt_lo"], t)
                for c in range(KC):
                    ins = pe.transpose(pT[:, c * P:(c + 1) * P], xn[:, u, c * P:(c + 1) * P], ident[:])
                ins.then_inc(S["xt_ps"], 1)

            transposes(0, 0)
            pe.wait_ge(S["c_dve"], 1)
            for k in range(4):
                o = pK[:, k * CH:(k + 1) * CH] if k < 3 else pV[:, 0:CH]
                pe.transpose(o[:, 0:P], frow[:, k, 0, :], ident[:])
                ins = pe.transpose(o[:, P:CH], frow[0:CH - P, k, 1, :], ident[0:CH - P, 0:CH - P])
            ins.then_inc(S["e_pe"], 1)

            def adj(j, r):
                pe.wait_ge(S["oh_dve"], j + 1)
                pe.wait_ge(S["oh_act"], j + 1)
                pe.wait_ge(S["oh_pool"], j + 1)
                if later(j, 1):
                    pe.wait_ge(S["a_acc"], j)
                for c in range(2):
                    for part in range(2):
                        ins = pe.matmul(pA[:, 0:T * WIN], Loh[:, r, c, part, :], Roh[:, r, c, :],
                                        start=(c + part == 0), stop=(c + part == 2))
                ins.then_inc(S["a_mm"], 1)

            outs = [(pQ, "q_mm", "q_er", 2), (pK, "k_mm", "k_er", 2), (pV, "v_mm", "v_lo", 1), (pH, "h_mm", "h_out", 1)]

            def kv(t, first, rows):
                pe.wait_ge(S["k_lo"], t + 1)
                pe.wait_ge(S["v_lo"], t + 1)
                for pr in range(PAIRS):
                    o = pKV[pr // 2][:, (pr % 2) * VC:(pr % 2 + 1) * VC]
                    for n, (x, y) in enumerate(((0, 0), (0, 1), (1, 0))):
                        ins = pe.matmul(o, khl[0:rows, x, pr * P:(pr + 1) * P], vhl[0:rows, y, pr, :],
                                        start=(first and pr % 2 == 0 and n == 0),
                                        stop=(rows < P and n == 2), skip_group_check=True)
                ins.then_inc(S["kv_mm"], 1)

            def two(i, first=False, last=False):
                at = [0]
                blocks = 0
                for u in range(2):
                    t = 2 * i + u
                    for k, (bank, done, free, per) in enumerate(outs):
                        if k == 0:
                            pe.wait_ge(S["xt_lo"], t + 1)
                        if k == 3 and not (last and u == 1):
                            transposes(t + 1, 1 - u)
                        if first and u == 0:
                            if k == 1:
                                pe.wait_ge(S["c_dve"], 2)
                                pe.matmul(pH[:, 0:CP], onesf[0:1, :], baserow[:], start=True, stop=True).then_inc(S["e_pe"], 1)
                            if k == 3:
                                pe.wait_ge(S["e_dve"], 1)
                            pe.wait_ge(S["w_lo2" if k in (1, 2) else "w_lo"], (1, 1, 2, 2)[k])
                        if not (first and u == 0):
                            pe.wait_ge(S[free], per * t)
                        for c in range(KC):
                            for n, (x, y) in enumerate(((0, 0), (0, 1), (1, 0))):
                                ins = pe.matmul(bank[:, :], xT[:, u, x, c, :], wsl[:, k, y, c, :],
                                                start=(c == 0 and n == 0), stop=(c == KC - 1 and n == 2))
                            if c == KC - 1:
                                ins.then_inc(S[done], 1)
                            blocks += 1
                            while at[0] < (blocks * CPI // 32 if not first else max(0, blocks - 16) * CPI // 16):
                                adj(CPI * i + at[0], at[0] % 3)
                                at[0] += 1
                    kv(t, first and u == 0, LAST if last and u == 1 else P)
                    if first and u == 0:
                        pe.wait_ge(S["rest_ok"], 1)
                        pe.matmul(pA[0:1, 0:1], outside[:], onesf[:, 0:1], start=True, stop=True).then_inc(S["rest_ps"], 1)
                        pe.wait_ge(S["flag_ok"], 1)

            two(0, first=True)
            with pe.Fori(1, ITER - 1) as i:
                two(i)
            two(ITER - 1, last=True)

            count_reg = pe.alloc_register("outside")
            pe.wait_ge(S["flag_ok"], 1)
            pe.load(count_reg, flagint[0:1, 0:1])
            with pe.If(pe.snap(count_reg, min_val=0, max_val=CH * P) > 0):
                with pe.Fori(0, NP // WIN) as w:
                    with pe.Fori(0, CP) as g:
                        pe.wait_ge(S["rest_oh"], CP * w + g + 1)
                        for c in range(2):
                            for part in range(2):
                                ins = pe.matmul(pA[:, 0:T * WIN], Loh[:, 0, c, part, :], Roh[:, 0, c, :],
                                                start=(c + part == 0), stop=(c + part == 2))
                        ins.then_inc(S["rest_mm"], 1)

            THREE = ((0, 0), (0, 1), (1, 0))
            pe.wait_ge(S["bd_ok"], 1)
            for c in range(KC):
                ins = pe.transpose(pT[:, c * P:(c + 1) * P], rt[:, c * P:(c + 1) * P], ident[:])
            ins.then_inc(S["kvt_ps"], 1)
            pe.wait_ge(S["q_er"], 2 * T)
            for p in range(PAIRS):
                ins = pe.matmul(pQ[:, p * P:(p + 1) * P], et[:, p * P:(p + 1) * P], ident[:], start=True, stop=True)
            ins.then_inc(S["ksb_ps"], 1)
            pe.wait_ge(S["dhl_lo"], 1)
            for x in range(2):
                for t in range(T):
                    ins = pe.matmul(pA[:, 2 * t:2 * t + 2], dhl[:, x, t * P:(t + 1) * P], ones2[:],
                                    start=(x + t == 0), stop=(x == 1), skip_group_check=True)
            ins.then_inc(S["deg_ps"], 1)
            def q_transposes(t, u, first=False):
                pe.wait_ge(S["qs_ok"], t + 1)
                if not first:
                    pe.wait_ge(S["qt_lo"], t)
                for c in range(KC):
                    ins = pe.transpose(pT[:, c * P:(c + 1) * P], (xn[:, 1, :], rt[:])[u][:, c * P:(c + 1) * P], ident[:])
                ins.then_inc(S["qt_ps"], 1)

            def aggregate(t, u, first=False):
                pe.wait_ge(S["ats_lo"], t + 1)
                if not first:
                    pe.wait_ge(S["x1_ok"], t - 1)
                for s_ in range(T):
                    if first and u == 0:
                        pe.wait_ge(S["g_lo"], s_ + 1)
                    for n, (x, y) in enumerate(THREE):
                        ins = pe.matmul(pG[u][:, :], ATs[:, u, x, s_, :], G[:, y, s_, :],
                                        start=(s_ + n == 0), stop=(s_ == T - 1 and n == 2))
                ins.then_inc(S["agg_mm"], 1)

            def mix(t, u, first=False):
                pe.wait_ge(S["qt_lo"], t + 1)
                if first:
                    pe.wait_ge(S["m_lo"], PAIRS)
                for c in range(KC):
                    for n, (x, y) in enumerate(THREE):
                        ins = pe.matmul(pM[u][:, :], xT[:, u, x, c, :], WO[:, y, c, :],
                                        start=(c + n == 0), stop=(c == KC - 1 and n == 2))
                ins.then_inc(S["mix_mm"], 1)

            aggregate(0, 0, True)
            pe.wait_ge(S["kvt_lo"], 1)
            pe.wait_ge(S["wo_lo"], 1)
            for p, bank in enumerate(mbank):
                pe.wait_ge(S["h_out"], T)
                pe.wait_ge(S["ksb_ok"], 1)
                for n, (x, y) in enumerate(THREE):
                    ins = pe.matmul(bank[:, :], xT[:, 0, x, p, :], WO[:, y, p, :], start=(n == 0), stop=(n == 2))
                ins.then_inc(S["m_mm"], 1)
            q_transposes(0, 0, True)
            aggregate(1, 1, True)
            q_transposes(1, 1)
            mix(0, 0, True)
            mix(1, 1)
            q_transposes(2, 0)
            with pe.Fori(1, ITER - 1) as i:
                for u in range(2):
                    aggregate(2 * i + u, u)
                    q_transposes(2 * i + u + 1, 1 - u)
                    mix(2 * i + u, u)
            aggregate(T - 2, 0)
            q_transposes(T - 1, 1)
            mix(T - 2, 0)
            aggregate(T - 1, 1)
            mix(T - 1, 1)

            for l in range(FFL):
                bank = wbank[l]
                if l == 0:
                    pe.wait_ge(S["fn_ok"], 2)
                if l == 4:
                    pe.wait_ge(S["x1_ok"], T - 1)
                if l == 5:
                    pe.wait_ge(S["fw_hi"], 1)
                if l == 6:
                    pe.wait_ge(S["fw_lo"], 1)
                thrice = 3 * REM
                if l == 0:
                    for pos in range(2):
                        pe.transpose(bank[0:20, pos * FM:pos * FM + P], N0[:, 0, pos, :], ident[:])
                        ins = pe.transpose(bank[0:20, pos * FM + P:(pos + 1) * FM], N0[0:thrice, 1, pos, :], ident[0:thrice, 0:thrice])
                elif l < FFL - 1:
                    pe.transpose(bank[:, 0:P], N1[:, l, 0:P], ident[:])
                    pe.transpose(bank[:, P:FM], N2[0:thrice, l, 0:P], ident[0:thrice, 0:thrice])
                    pe.transpose(bank[0:FX, FM:FM + P], N1[:, l, P:FK], ident[:])
                    ins = pe.transpose(bank[0:FX, FM + P:2 * FM], N2[0:thrice, l, P:FK], ident[0:thrice, 0:thrice])
                else:
                    pe.transpose(bank[:, 0:REM], N1[0:REM, l, 0:P], ident[0:REM, 0:REM])
                    ins = pe.transpose(bank[0:FX, REM:2 * REM], N1[0:REM, l, P:FK], ident[0:REM, 0:REM])
                ins.then_inc(S["fw_ps"], 1)
            pe.wait_ge(S["f20_ok"], 1)
            pe.wait_ge(S["pads_ok"], 3)
            for k, bank in enumerate((pK, pV, pH)):
                if k == 2:
                    pe.wait_ge(S["fw_lo"], 4)
                for t in range(4 * k, min(4 * k + 4, T)):
                    ins = pe.transpose(bank[0:20, (t % 4) * P:(t % 4 + 1) * P], F20[:, t, :], ident[:])
                ins.then_inc(S["ft_ps"], 1)
            pe.wait_ge(S["fw_lo"], FFL - 1)
            pe.wait_ge(S["fw_hi"], FFL)

            for k in range(STEPS - FC):
                l, c = divmod(k, FC)
                m_, r_ = fmain[k % 3], frest[k % 3]
                if k < 3:
                    pe.wait_ge(S["ft_ok"], 3)
                else:
                    pe.wait_ge(S["f_lo"], k - 2)
                if l == 0:
                    for pos in range(2):
                        w, x = FW0[0:20, pos], FT[0:20, c * FN:(c + 1) * FN]
                        pe.matmul(m_[:, pos * FN:(pos + 1) * FN], w[:, 0:P], x, start=True, stop=True)
                        ins = pe.matmul(r_[0:3 * REM, pos * FN:(pos + 1) * FN], w[:, P:FM], x, start=True, stop=True)
                else:
                    for o, w in ((m_[:, :], slice(0, P)), (r_[0:3 * REM, :], slice(P, FM))):
                        for n, (x, y) in enumerate(THREE):
                            pe.matmul(o, FWm[:, y, l - 1, w], H[:, x, c, :], start=(n == 0), stop=False)
                        ins = pe.matmul(o, FWx[0:FX, l - 1, w], Rr[0:FX, c, :], start=False, stop=True)
                ins.then_inc(S["f_mm"], 1)
            for c in range(FC):
                pe.wait_ge(S["f_lo"], STEPS - 2 * FC + c + 1)
                for q in range(4):
                    o = pKV[0][:, (4 * c + q) * 2:(4 * c + q) * 2 + 2]
                    sl = slice(q * P, (q + 1) * P)
                    pe.matmul(o, H[:, 0, c, sl], w6[:, 0:2], start=True, stop=False)
                    pe.matmul(o, H[:, 1, c, sl], w6[:, 2:4], start=False, stop=False)
                    ins = pe.matmul(o, Rr[0:FX, c, sl], w6x[0:FX, :], start=False, stop=True)
            ins.then_inc(S["f6_mm"], 1)

            def turn(t, u, first=False):
                pe.wait_ge(S["n_xn"], t + 1 + after["n_xn"])
                if not first:
                    pe.wait_ge(S["n_lo"], t + after["n_lo"])
                for c in range(KC):
                    ins = pe.transpose(pT[:, c * P:(c + 1) * P], xn[:, u, c * P:(c + 1) * P], ident[:])
                ins.then_inc(S["n_ps"], 1)

            def product(o, u, w, done):
                for c in range(KC):
                    for n, (x, y) in enumerate(THREE):
                        ins = pe.matmul(o, xT[:, u, x, c, :], w[:, y, c, :], start=(c + n == 0), stop=(c == KC - 1 and n == 2))
                ins.then_inc(S[done], 1)

            def tile1(t, u, first=False, last=False):
                pe.wait_ge(S["n_lo"], t + 1 + after["n_lo"])
                if first:
                    pe.wait_ge(S["q1_lo"], 1 + after["q1_lo"])
                else:
                    pe.wait_ge(S["nq_sub"], t + after["nq_sub"])
                product(pQ[:, :], u, Wq, "nq_mm")
                if first:
                    pe.wait_ge(S["k1_lo"], 1 + after["k1_lo"])
                else:
                    pe.wait_ge(S["nk_er"], 2 * t + after["nk_er"])
                if not last:
                    turn(t + 1, 1 - u)
                product(pK[:, :], u, Wk, "nk_mm")
                if first:
                    pe.wait_ge(S["u1_lo"], 1 + after["u1_lo"])
                else:
                    pe.wait_ge(S["nu_lo"], t + after["nu_lo"])
                product(pV[:, 0:RANK], u, Wu, "nu_mm")

            turn(0, 0, True)
            tile1(0, 0, True)
            tile1(1, 1)
            with pe.Fori(1, ITER - 1) as i:
                for u in range(2):
                    tile1(2 * i + u, u)
            tile1(T - 2, 0)
            tile1(T - 1, 1, last=True)

            pe.wait_ge(S["kmax_ok"], T)
            pe.wait_ge(S["n_lo"], T + after["n_lo"])
            for c in range(KC):
                ins = pe.transpose(pT[:, c * P:(c + 1) * P], kmax[:, c * P:(c + 1) * P], ident[:])
            ins.then_inc(S["cm_ps"], 1)
            pe.wait_ge(S["cm_ok"], 1 + after["cm_ok"])
            for p in range(PAIRS):
                ins = pe.matmul(pA[:, p * P:(p + 1) * P], et[:, p * P:(p + 1) * P], ident[:], start=True, stop=True)
            ins.then_inc(S["cmb_ps"], 1)

            zbank = (pK, pV, pH, pQ)

            def keys(t, u, first=False, rows=P):
                pe.wait_ge(S["z_xlo"], t + 1)
                pe.wait_ge(S["z_klo"], t + 1 + after["z_klo"])
                for b, bank in enumerate(zbank):
                    for n, (x, y) in enumerate(THREE):
                        ins = pe.matmul(bank[:, :], khl2[0:rows, u, x, b * P:(b + 1) * P], xT[0:rows, u, y].rearrange("p c n -> p (c n)"),
                                        start=(first and n == 0), stop=(rows < P and n == 2), skip_group_check=True)
                    for x in range(2):
                        ins = pe.matmul(pKV[0][:, 2 * b:2 * b + 2], khl2[0:rows, u, x, b * P:(b + 1) * P], ones2[0:rows, :],
                                        start=(first and b + x == 0), stop=(rows < P and x == 1), skip_group_check=True)
                ins.then_inc(S["z_mm"], 1)

            pe.wait_ge(S["c1"], 5)
            keys(0, 0, True)
            keys(1, 1)
            with pe.Fori(1, ITER - 1) as i:
                for u in range(2):
                    keys(2 * i + u, u)
            keys(T - 2, 0)
            keys(T - 1, 1, rows=LAST)

            pe.wait_ge(S["zs_a"], 2)
            pe.wait_ge(S["zs_d"], 2)
            for c, bank in enumerate((pT, pA, pKV[0], pKV[1])):
                for b, z in enumerate((xn[:, 0, :], xn[:, 1, :], et[:], rt[:])):
                    ins = pe.transpose(bank[:, b * P:(b + 1) * P], z[:, c * P:(c + 1) * P], ident[:])
            ins.then_inc(S["zt_ps"], 1)
            for p in range(PAIRS):
                for c in range(KC):
                    if p == 0:
                        pe.wait_ge(S["zt_lo"], c + 1 + after["zt_lo"])
                    for n, (x, y) in enumerate(THREE):
                        cols = slice(p * P, (p + 1) * P)
                        ins = pe.matmul(pK[:, cols], Wv[:, x, c, cols], ZT[:, y, c, cols],
                                        start=(c + n == 0), stop=(c == KC - 1 and n == 2))
            ins.then_inc(S["kt_mm"], 1)
            pe.wait_ge(S["kt_lo"], 2)
            pe.wait_ge(S["p1_lo"], KC)
            for p, bank in enumerate((pV, pH, pQ, pT)):
                for n, (x, y) in enumerate(THREE):
                    ins = pe.matmul(bank[:, :], xT[:, 0, x, p, :], Wp[:, y, p, :], start=(n == 0), stop=(n == 2))
                ins.then_inc(S["mw_mm"], 1)

            def turn2(t, u, first=False):
                pe.wait_ge(S["r2_qs"], t + 1 + after["r2_qs"])
                if not first:
                    pe.wait_ge(S["r2_lo"], t + after["r2_lo"])
                for c in range(KC):
                    ins = pe.transpose(pT[:, c * P:(c + 1) * P], (et, rt)[u][:, c * P:(c + 1) * P], ident[:])
                ins.then_inc(S["r2_ps"], 1)

            def turn_weights(t, u, c):
                k = 3 * t + c
                if k >= 2:
                    pe.wait_ge(S["a2_lo"], k - 1)
                for s_ in range(4 * c, min(4 * c + 4, T)):
                    ins = pe.transpose(chunk_bank(u, c)[:, (s_ % 4) * P:(s_ % 4 + 1) * P], AT[:, t, s_ * P:(s_ + 1) * P], ident[:])
                ins.then_inc(S["a2_ps"], 1)

            def low_rank(t, u):
                pe.wait_ge(S["a2_lo"], 3 * t + 3)
                if t >= 1:
                    pe.wait_ge(S["g2_lo"], t + after["g2_lo"])
                o = pKV[0]
                for s_ in range(T):
                    pe.matmul(o[:, 0:P], uhl[:, s_, :], ATs[:, u, 0, s_, :], start=(s_ == 0), stop=False, skip_group_check=True)
                    ins = pe.matmul(o[0:RANK, 0:P], uhl[:, s_, 0:RANK], ATs[:, u, 1, s_, :], start=False, stop=(s_ == T - 1), skip_group_check=True)
                ins.then_inc(S["a2_mm"], 1)

            def support(t, u, first=False):
                pe.wait_ge(S["g2_lo"], t + 1 + after["g2_lo"])
                if not first:
                    pe.wait_ge(S["x3_ok"], t - 1 + after["x3_ok"])
                for n, (x, y) in enumerate(THREE):
                    pe.matmul(pG[u][:, :], agT[:, u, x, :], Vt[:, y, :], start=(n == 0), stop=False)
                pe.matmul(pG[u][:, :], rows1[:, 0, :], b2[0:2, 0, :], start=False, stop=True).then_inc(S["s2_mm"], 1)

            def mix2(t, u):
                pe.wait_ge(S["r2_lo"], t + 1 + after["r2_lo"])
                for c in range(KC):
                    for n, (x, y) in enumerate(THREE):
                        pe.matmul(pM[u][:, :], xT[:, u, x, c, :], MW[:, y, c, :], start=(c + n == 0), stop=False)
                pe.matmul(pM[u][:, :], rows1[:, 0, :], b2[0:2, 1, :], start=False, stop=True).then_inc(S["m2_mm"], 1)

            for t in range(2):
                for c in range(3):
                    turn_weights(t, t, c)
            low_rank(0, 0)
            pe.wait_ge(S["mw_lo"], PAIRS + after["mw_lo"])
            turn2(0, 0, True)
            pe.wait_ge(S["vt_lo"], 1)
            pe.wait_ge(S["b2_ok"], 1)
            for t in range(T):
                u = t % 2
                if t + 2 < T:
                    turn_weights(t + 2, u, 0)
                    turn_weights(t + 2, u, 1)
                if t + 1 < T:
                    low_rank(t + 1, 1 - u)
                if t + 2 < T:
                    turn_weights(t + 2, u, 2)
                if t + 1 < T:
                    turn2(t + 1, 1 - u)
                support(t, u, t < 2)
                mix2(t, u)

            pe.wait_ge(S["ld_f1"], 64 + after["ld_f1"])
            pe.wait_ge(S["g2_lo"], T + after["g2_lo"])
            pe.wait_ge(S["r2_lo"], T + after["r2_lo"])
            for k, bank in enumerate((pKV[0], pT)):
                for c in range(2):
                    for b in range(2):
                        ins = pe.transpose(bank[:, c * HALF + b * P:c * HALF + (b + 1) * P], f1r[:, b, (2 * k + c) * P:(2 * k + c + 1) * P], ident[:])
                ins.then_inc(S["f1_ps"], 1)
            for hb in range(2):
                for b in range(2):
                    ins = pe.transpose(pKV[1][:, hb * HALF + b * P:hb * HALF + (b + 1) * P], f2r[:, b, hb * P:(hb + 1) * P], ident[:])
            ins.then_inc(S["f2_ps"], 1)
            pe.wait_ge(S["pt_lo"], 1)
            pe.wait_ge(S["f1_lo"], 2)
            for ib in range(2):
                for c in range(KC):
                    for n, (x, y) in enumerate(THREE):
                        ins = pe.matmul(pA[:, ib * HALF:(ib + 1) * HALF], PTh[:, x, c, ib * P:(ib + 1) * P], f1T[:, y, c, :],
                                        start=(c + n == 0), stop=(c == KC - 1 and n == 2))
            ins.then_inc(S["w1_mm"], 1)
            for g in range(3):
                n = min(4, T - 4 * g)
                pe.wait_ge(S["s_lo"], g + 1)
                for k in range(n):
                    for ib in range(2):
                        for x in range(2):
                            ins = pe.matmul((pK, pV, pH)[g][:, (2 * k + ib) * DH:(2 * k + ib + 1) * DH], shl[:, x, 4 * g + k, ib * P:(ib + 1) * P],
                                            pairq[:], start=(x == 0), stop=(x == 1))
                ins.then_inc(S["ll_mm"], 1)
            pe.wait_ge(S["w1_lo"], 1)
            for g in range(3):
                n = min(4, T - 4 * g) * DH
                r = slice(4 * g * DH, 4 * g * DH + n)
                pe.wait_ge(S["ll_lo"], g + 1)
                for hb in range(2):
                    for ib in range(2):
                        for m, (x, y) in enumerate(THREE):
                            ins = pe.matmul((pQ, pA, pT)[g][:, hb * HALF:hb * HALF + n], W1[:, x, ib, hb * P:(hb + 1) * P], llT[:, y, ib, r],
                                            start=(ib + m == 0), stop=(ib == 1 and m == 2))
                ins.then_inc(S["hh_mm"], 1)
            pe.wait_ge(S["b3_ok"], 1)
            pe.wait_ge(S["f2_lo"], 1)
            for t in range(T):
                o = obank[t % 4][:, 0:HALF]
                if t >= 4:
                    pe.wait_ge(S["o_ok"], t - 3)
                pe.matmul(o, rows1[:, 1, :], b3[0:2, :], start=True, stop=False)
                for x in range(2):
                    pe.matmul(o, pairm[:], shl[:, x, t, :], start=False, stop=False)
                pe.wait_ge(S["hh_lo"], 2 * (t // 4) + 2)
                for hb in range(2):
                    for n, (x, y) in enumerate(THREE):
                        ins = pe.matmul(o, hT[:, x, hb, t * P:(t + 1) * P], f2T[:, y, hb, :], start=False, stop=(hb == 1 and n == 2))
                ins.then_inc(S["o_mm"], 1)


INPUTS = ['x', 'src', 'dst', 'edge_weight', 'L0_gnn_W', 'L0_gnn_b', 'L0_mix_w_qkv', 'L0_mix_w_out', 'L0_mix_b_out', 'L0_ffn_W', 'L0_ffn_b', 'L1_gnn_U', 'L1_gnn_s', 'L1_gnn_Vt', 'L1_gnn_bias', 'L1_mix_w_qkv', 'L1_mix_w_proj', 'L1_mix_b_proj', 'L1_ffn_fc1_w', 'L1_ffn_fc1_b', 'L1_ffn_fc2_w', 'L1_ffn_fc2_b']


def kernel(**inputs):
    import numpy as _np
    import concourse.bacc as _bacc
    from concourse import mybir as _mybir
    from concourse.bass_utils import run_bass_kernel_spmd as _run

    nc = _bacc.Bacc("TRN2", target_bir_lowering=False, num_devices=1)
    arrays, aps = {}, {}
    for name in INPUTS:
        v = _np.ascontiguousarray(inputs[name])
        arrays[f"in_{name}"] = v
        aps[name] = nc.dram_tensor(f"in_{name}", v.shape, _mybir.dt.from_np(v.dtype), kind="ExternalInput").ap()
    arrays["interp"] = interpolation()
    aps["interp"] = nc.dram_tensor("interp", (D, HALF), _mybir.dt.float32, kind="ExternalInput").ap()
    out = nc.dram_tensor("out", (N, D), _mybir.dt.float32, kind="ExternalOutput").ap()
    build(nc, aps, out)
    r = _run(nc, [arrays], core_ids=[0])
    return r.results[0]["out"]
```
